# Optimizing a Trainium2 kernel written in Bass

```python
import numpy as np
import jax
import jax.numpy as jnp

def _softmax(x, axis=-1):
    return jax.nn.softmax(x, axis=axis)
def _gelu(x):
    return jax.nn.gelu(x, approximate=True)
def _silu(x):
    return jax.nn.silu(x)
def _sigmoid(x):
    return jax.nn.sigmoid(x)
def _layernorm(x, axis=-1, eps=1e-5):
    m = jnp.mean(x, axis=axis, keepdims=True)
    v = jnp.var(x, axis=axis, keepdims=True)
    return (x - m) / jnp.sqrt(v + eps)
def _scatter_add(tgt, idx, src, axis=0):
    return tgt.at[idx].add(src)
def _segment_sum(src, seg, n):
    return jax.ops.segment_sum(src, seg, n)

kernel_name = 'mk_conv_seq_d2_conv_nchw64_dc40f8'

def setup_inputs(seed: int = 0):
    np.random.seed(seed)
    _w = jnp.asarray
    def _rec_inputs():
        import jax
        import jax.numpy as jnp
        _gk = jax.random.key(seed)
        x = 0.00045 + 0.9999 * jax.random.normal(jax.random.fold_in(_gk, 1), (4, 64, 80, 80), jnp.float32)
        return x
    x = _rec_inputs()
    def _L0_conv_setup():
        import jax, jax.numpy as jnp
        import numpy as np
        KSIZE = 3
        STRIDE = 1
        RATE = 2
        SOFTMAX_SCALE = 10.0
        ESCAPE = 0.0001

        def _same_pad(x, k, s):
            H, W = (x.shape[2], x.shape[3])
            oh, ow = (-(-H // s), -(-W // s))
            ph = max((oh - 1) * s + k - H, 0)
            pw = max((ow - 1) * s + k - W, 0)
            return jnp.pad(x, ((0, 0), (0, 0), (ph // 2, ph - ph // 2), (pw // 2, pw - pw // 2)))

        def _extract_patches(x, k, s):
            xp = _same_pad(x, k, s)
            B, C, H, W = xp.shape
            Ho, Wo = ((H - k) // s + 1, (W - k) // s + 1)
            cols = [xp[:, :, u:u + (Ho - 1) * s + 1:s, v:v + (Wo - 1) * s + 1:s] for u in range(k) for v in range(k)]
            p = jnp.stack(cols, axis=-1)
            p = p.transpose(0, 2, 3, 1, 4).reshape(B, Ho * Wo, C, k, k)
            return (p, Ho, Wo)

        def _contextual(b, mask):
            B, C, H, W = b.shape
            kernel = 2 * RATE
            raw_w, Hr, Wr = _extract_patches(b, kernel, RATE * STRIDE)
            f = b[:, :, ::RATE, ::RATE]
            m_s = mask[:, :, ::RATE, ::RATE]
            w, Hs, Ws = _extract_patches(f, KSIZE, STRIDE)
            L = Hs * Ws
            m, _, _ = _extract_patches(m_s, KSIZE, STRIDE)
            mm = (jnp.mean(m[0], axis=(1, 2, 3)) == 0.0).astype(b.dtype)[None, :, None]
            norm = jnp.sqrt(jnp.sum(w * w, axis=(2, 3, 4), keepdims=True))
            wn = (w / jnp.maximum(norm, ESCAPE)).reshape(B, L, C * KSIZE * KSIZE)
            xf = w.reshape(B, L, C * KSIZE * KSIZE)
            yi = jnp.einsum('bpd,bld->blp', xf, wn)
            yi = yi * mm
            yi = jax.nn.softmax(yi * SOFTMAX_SCALE, axis=1)
            yi = yi * mm
            patches = jnp.einsum('blp,bld->bpd', yi, raw_w.reshape(B, L, C * kernel * kernel))
            Pc = patches.reshape(B, Hs, Ws, C, kernel, kernel).transpose(0, 3, 4, 5, 1, 2)
            pad = 1
            Hp, Wp = ((Hs - 1) * RATE + kernel, (Ws - 1) * RATE + kernel)
            out = jnp.zeros((B, C, Hp, Wp), b.dtype)
            for u in range(kernel):
                for v in range(kernel):
                    out = out.at[:, :, u:u + (Hs - 1) * RATE + 1:RATE, v:v + (Ws - 1) * RATE + 1:RATE].add(Pc[:, :, u, v])
            out = out[:, :, pad:Hp - pad, pad:Wp - pad]
            return out / 4.0
        key = jax.random.key(seed)
        b = jax.random.normal(key, (4, 64, 80, 80), dtype=jnp.float32)
        mask = jnp.zeros((1, 1, 80, 80), dtype=jnp.float32)
        return {'b': b, 'mask': mask}
    _L0_conv_all = _L0_conv_setup()
    _L0_conv_in = {k: v for k, v in _L0_conv_all.items() if k in ('mask', )}
    del _L0_conv_all

    def _L1_conv_setup():
        import jax, jax.numpy as jnp
        import numpy as np
        KSIZE = 3
        STRIDE = 1
        RATE = 2
        SOFTMAX_SCALE = 10.0
        ESCAPE = 0.0001

        def _same_pad(x, k, s):
            H, W = (x.shape[2], x.shape[3])
            oh, ow = (-(-H // s), -(-W // s))
            ph = max((oh - 1) * s + k - H, 0)
            pw = max((ow - 1) * s + k - W, 0)
            return jnp.pad(x, ((0, 0), (0, 0), (ph // 2, ph - ph // 2), (pw // 2, pw - pw // 2)))

        def _extract_patches(x, k, s):
            xp = _same_pad(x, k, s)
            B, C, H, W = xp.shape
            Ho, Wo = ((H - k) // s + 1, (W - k) // s + 1)
            cols = [xp[:, :, u:u + (Ho - 1) * s + 1:s, v:v + (Wo - 1) * s + 1:s] for u in range(k) for v in range(k)]
            p = jnp.stack(cols, axis=-1)
            p = p.transpose(0, 2, 3, 1, 4).reshape(B, Ho * Wo, C, k, k)
            return (p, Ho, Wo)

        def _contextual(b, mask):
            B, C, H, W = b.shape
            kernel = 2 * RATE
            raw_w, Hr, Wr = _extract_patches(b, kernel, RATE * STRIDE)
            f = b[:, :, ::RATE, ::RATE]
            m_s = mask[:, :, ::RATE, ::RATE]
            w, Hs, Ws = _extract_patches(f, KSIZE, STRIDE)
            L = Hs * Ws
            m, _, _ = _extract_patches(m_s, KSIZE, STRIDE)
            mm = (jnp.mean(m[0], axis=(1, 2, 3)) == 0.0).astype(b.dtype)[None, :, None]
            norm = jnp.sqrt(jnp.sum(w * w, axis=(2, 3, 4), keepdims=True))
            wn = (w / jnp.maximum(norm, ESCAPE)).reshape(B, L, C * KSIZE * KSIZE)
            xf = w.reshape(B, L, C * KSIZE * KSIZE)
            yi = jnp.einsum('bpd,bld->blp', xf, wn)
            yi = yi * mm
            yi = jax.nn.softmax(yi * SOFTMAX_SCALE, axis=1)
            yi = yi * mm
            patches = jnp.einsum('blp,bld->bpd', yi, raw_w.reshape(B, L, C * kernel * kernel))
            Pc = patches.reshape(B, Hs, Ws, C, kernel, kernel).transpose(0, 3, 4, 5, 1, 2)
            pad = 1
            Hp, Wp = ((Hs - 1) * RATE + kernel, (Ws - 1) * RATE + kernel)
            out = jnp.zeros((B, C, Hp, Wp), b.dtype)
            for u in range(kernel):
                for v in range(kernel):
                    out = out.at[:, :, u:u + (Hs - 1) * RATE + 1:RATE, v:v + (Ws - 1) * RATE + 1:RATE].add(Pc[:, :, u, v])
            out = out[:, :, pad:Hp - pad, pad:Wp - pad]
            return out / 4.0
        key = jax.random.key(seed)
        b = jax.random.normal(key, (4, 64, 80, 80), dtype=jnp.float32)
        mask = jnp.zeros((1, 1, 80, 80), dtype=jnp.float32)
        return {'b': b, 'mask': mask}
    _L1_conv_all = _L1_conv_setup()
    _L1_conv_in = {k: v for k, v in _L1_conv_all.items() if k in ('mask', )}
    del _L1_conv_all

    return {
        "x": x,
        "L0_conv_mask": _L0_conv_in["mask"],
        "L1_conv_mask": _L1_conv_in["mask"],
    }

def reference(x, L0_conv_mask, L1_conv_mask):
    import jax
    import jax.numpy as jnp
    def _L0_conv_ref(b, mask):
        import jax, jax.numpy as jnp
        import numpy as np
        KSIZE = 3
        STRIDE = 1
        RATE = 2
        SOFTMAX_SCALE = 10.0
        ESCAPE = 0.0001

        def _same_pad(x, k, s):
            H, W = (x.shape[2], x.shape[3])
            oh, ow = (-(-H // s), -(-W // s))
            ph = max((oh - 1) * s + k - H, 0)
            pw = max((ow - 1) * s + k - W, 0)
            return jnp.pad(x, ((0, 0), (0, 0), (ph // 2, ph - ph // 2), (pw // 2, pw - pw // 2)))

        def _extract_patches(x, k, s):
            xp = _same_pad(x, k, s)
            B, C, H, W = xp.shape
            Ho, Wo = ((H - k) // s + 1, (W - k) // s + 1)
            cols = [xp[:, :, u:u + (Ho - 1) * s + 1:s, v:v + (Wo - 1) * s + 1:s] for u in range(k) for v in range(k)]
            p = jnp.stack(cols, axis=-1)
            p = p.transpose(0, 2, 3, 1, 4).reshape(B, Ho * Wo, C, k, k)
            return (p, Ho, Wo)

        def _contextual(b, mask):
            B, C, H, W = b.shape
            kernel = 2 * RATE
            raw_w, Hr, Wr = _extract_patches(b, kernel, RATE * STRIDE)
            f = b[:, :, ::RATE, ::RATE]
            m_s = mask[:, :, ::RATE, ::RATE]
            w, Hs, Ws = _extract_patches(f, KSIZE, STRIDE)
            L = Hs * Ws
            m, _, _ = _extract_patches(m_s, KSIZE, STRIDE)
            mm = (jnp.mean(m[0], axis=(1, 2, 3)) == 0.0).astype(b.dtype)[None, :, None]
            norm = jnp.sqrt(jnp.sum(w * w, axis=(2, 3, 4), keepdims=True))
            wn = (w / jnp.maximum(norm, ESCAPE)).reshape(B, L, C * KSIZE * KSIZE)
            xf = w.reshape(B, L, C * KSIZE * KSIZE)
            yi = jnp.einsum('bpd,bld->blp', xf, wn)
            yi = yi * mm
            yi = jax.nn.softmax(yi * SOFTMAX_SCALE, axis=1)
            yi = yi * mm
            patches = jnp.einsum('blp,bld->bpd', yi, raw_w.reshape(B, L, C * kernel * kernel))
            Pc = patches.reshape(B, Hs, Ws, C, kernel, kernel).transpose(0, 3, 4, 5, 1, 2)
            pad = 1
            Hp, Wp = ((Hs - 1) * RATE + kernel, (Ws - 1) * RATE + kernel)
            out = jnp.zeros((B, C, Hp, Wp), b.dtype)
            for u in range(kernel):
                for v in range(kernel):
                    out = out.at[:, :, u:u + (Hs - 1) * RATE + 1:RATE, v:v + (Ws - 1) * RATE + 1:RATE].add(Pc[:, :, u, v])
            out = out[:, :, pad:Hp - pad, pad:Wp - pad]
            return out / 4.0
        return _contextual(b, mask)

    def _L1_conv_ref(b, mask):
        import jax, jax.numpy as jnp
        import numpy as np
        KSIZE = 3
        STRIDE = 1
        RATE = 2
        SOFTMAX_SCALE = 10.0
        ESCAPE = 0.0001

        def _same_pad(x, k, s):
            H, W = (x.shape[2], x.shape[3])
            oh, ow = (-(-H // s), -(-W // s))
            ph = max((oh - 1) * s + k - H, 0)
            pw = max((ow - 1) * s + k - W, 0)
            return jnp.pad(x, ((0, 0), (0, 0), (ph // 2, ph - ph // 2), (pw // 2, pw - pw // 2)))

        def _extract_patches(x, k, s):
            xp = _same_pad(x, k, s)
            B, C, H, W = xp.shape
            Ho, Wo = ((H - k) // s + 1, (W - k) // s + 1)
            cols = [xp[:, :, u:u + (Ho - 1) * s + 1:s, v:v + (Wo - 1) * s + 1:s] for u in range(k) for v in range(k)]
            p = jnp.stack(cols, axis=-1)
            p = p.transpose(0, 2, 3, 1, 4).reshape(B, Ho * Wo, C, k, k)
            return (p, Ho, Wo)

        def _contextual(b, mask):
            B, C, H, W = b.shape
            kernel = 2 * RATE
            raw_w, Hr, Wr = _extract_patches(b, kernel, RATE * STRIDE)
            f = b[:, :, ::RATE, ::RATE]
            m_s = mask[:, :, ::RATE, ::RATE]
            w, Hs, Ws = _extract_patches(f, KSIZE, STRIDE)
            L = Hs * Ws
            m, _, _ = _extract_patches(m_s, KSIZE, STRIDE)
            mm = (jnp.mean(m[0], axis=(1, 2, 3)) == 0.0).astype(b.dtype)[None, :, None]
            norm = jnp.sqrt(jnp.sum(w * w, axis=(2, 3, 4), keepdims=True))
            wn = (w / jnp.maximum(norm, ESCAPE)).reshape(B, L, C * KSIZE * KSIZE)
            xf = w.reshape(B, L, C * KSIZE * KSIZE)
            yi = jnp.einsum('bpd,bld->blp', xf, wn)
            yi = yi * mm
            yi = jax.nn.softmax(yi * SOFTMAX_SCALE, axis=1)
            yi = yi * mm
            patches = jnp.einsum('blp,bld->bpd', yi, raw_w.reshape(B, L, C * kernel * kernel))
            Pc = patches.reshape(B, Hs, Ws, C, kernel, kernel).transpose(0, 3, 4, 5, 1, 2)
            pad = 1
            Hp, Wp = ((Hs - 1) * RATE + kernel, (Ws - 1) * RATE + kernel)
            out = jnp.zeros((B, C, Hp, Wp), b.dtype)
            for u in range(kernel):
                for v in range(kernel):
                    out = out.at[:, :, u:u + (Hs - 1) * RATE + 1:RATE, v:v + (Ws - 1) * RATE + 1:RATE].add(Pc[:, :, u, v])
            out = out[:, :, pad:Hp - pad, pad:Wp - pad]
            return out / 4.0
        return _contextual(b, mask)

    def _gn(v, G=32, eps=1e-5):
        B_, C_, H_, W_ = v.shape
        g = v.reshape(B_, G, C_ // G, H_, W_)
        m = jnp.mean(g, axis=(2, 3, 4), keepdims=True)
        s = jnp.var(g, axis=(2, 3, 4), keepdims=True)
        return ((g - m) / jnp.sqrt(s + eps)).reshape(v.shape)

    def _ln_c(v, eps=1e-6):
        m = jnp.mean(v, axis=1, keepdims=True)
        s = jnp.var(v, axis=1, keepdims=True)
        return (v - m) / jnp.sqrt(s + eps)

    def _ln_t(v, eps=1e-5):
        m = jnp.mean(v, axis=-1, keepdims=True)
        s = jnp.var(v, axis=-1, keepdims=True)
        return (v - m) / jnp.sqrt(s + eps)

    def _to_tokens(v):
        B_, C_, H_, W_ = v.shape
        return v.reshape(B_, C_, H_ * W_).transpose(0, 2, 1)
    def _from_tokens(t, like):
        B_, C_, H_, W_ = like.shape
        return t.transpose(0, 2, 1).reshape(B_, C_, H_, W_)

    x = _L0_conv_ref(x, L0_conv_mask)
    x = _L1_conv_ref(x, L1_conv_mask)
    return x


_drawn_inputs = setup_inputs


def setup_inputs(seed=0):
    import zlib

    import numpy as np

    out = dict(_drawn_inputs(seed))
    spreads = {}
    factors = {}
    for name, (base, spread) in spreads.items():
        noise = np.random.default_rng([zlib.crc32(name.encode()), seed]).standard_normal(out[name].shape)
        drawn = base * np.exp(spread * noise) if base else spread * noise
        out[name] = jnp.asarray(drawn.astype(out[name].dtype))
    for name, factor in factors.items():
        out[name] = (out[name] * factor).astype(out[name].dtype)
    return out
```

```python
from contextlib import ExitStack

import concourse.bass as bass
from concourse import mybir

F32 = mybir.dt.float32
F16 = mybir.dt.float16
ALU = mybir.AluOpType
ACT = mybir.ActivationFunctionType
AX = mybir.AxisListType

LAYERS, IMAGES, C, SIDE = 2, 4, 64, 80
UNITS = LAYERS * IMAGES
HALF = SIDE // 2
STRIPS, TILES = 3, 14
PITCH = HALF + 2
TW = STRIPS * PITCH
FROWS = TILES + 3
FLEN = FROWS * TW + 4
GLEN = (TILES + 2) * TW
SLOTS = TILES + 1
CHUNKS = [(0, 4, 4), (4, 4, 4), (8, 3, 3), (11, 3, 4)]
NK = len(CHUNKS)
ZSCALE = 4096.0
BIG = 1.0e30
FREE = 2


def contextual_attention(nc, x, mask0, mask1, ident, valid, out):
    mid = nc.dram_tensor("mid", (IMAGES, C, SIDE, SIDE), F32, kind="Internal").ap()

    with ExitStack() as ctx:
        def sb(name, shape, dt):
            return ctx.enter_context(nc.sbuf_tensor(name, shape, dt))

        def ps(name, shape):
            return ctx.enter_context(nc.psum_tensor(name, shape, F32))

        def sem(name):
            return ctx.enter_context(nc.semaphore(name))

        G = sb("G", [TW, TILES * GLEN], F32)
        HL = sb("HL", [128, FLEN], F16)
        LH = sb("LH", [128, FLEN], F16)
        H1 = sb("H1", [128, FLEN], F16)
        HV = sb("HV", [128, FLEN], F16)
        XP = sb("XP", [128, TILES * STRIPS, 2 * PITCH], F32)
        Bh = sb("Bh", [TW, TILES * 2 * 128], F16)
        Bl = sb("Bl", [TW, TILES * 2 * 128], F16)
        SQ = sb("SQ", [128, FLEN], F32)
        BX = sb("BX", [128, FLEN], F32)
        BC = sb("BC", [TW, SLOTS * TW], F32)
        S = sb("S", [TW, FREE, 4 * TW], F32)
        SH = sb("SH", [TW, FREE, 4 * TW], F32)
        SHJ = sb("SHJ", [TW, 4 * TW], F32)
        Z = sb("Z", [TW, FREE, 4 * TW], F32)
        Zh = sb("Zh", [TW, FREE, 4 * TW], F16)
        Zl = sb("Zl", [TW, FREE, 4 * TW], F16)
        OSB = sb("OSB", [128, 4 * STRIPS, 2 * PITCH], F32)
        idn = sb("idn", [128, 128], F32)
        ones = sb("ones", [128, 1], F32)
        vld = sb("vld", [TW, TILES], F32)
        big = sb("big", [TW, TILES], F32)
        mm20 = sb("mm20", [TW, UNITS * TILES], F32)
        nb = sb("nb", [TW, UNITS * TILES], F32)
        mmc = sb("mmc", [TW, LAYERS, TILES], F32)
        nsq = sb("nsq", [TW, TILES], F32)
        root = sb("root", [TW, TILES], F32)
        quo = sb("quo", [TW, TILES], F32)
        nrm2 = sb("nrm2", [TW, TILES], F32)
        rcp = sb("rcp", [TW, TILES], F32)
        R = sb("R", [TW, TILES], F32)
        mx = sb("mx", [TW, FREE], F32)
        nm = sb("nm", [TW, NK * TILES], F32)
        sg = sb("sg", [TW, (NK + 1) * TILES], F32)
        nM = sb("nM", [TW, TILES], F32)
        df = sb("df", [TW, NK * TILES], F32)
        ed = sb("ed", [TW, NK * TILES], F32)
        tot = sb("tot", [TW, TILES], F32)
        lns = sb("lns", [TW, TILES], F32)
        lse = sb("lse", [TW, TILES], F32)

        psG = ps("psG", [128, FREE, 512])
        psO = ps("psO", [128, FREE, 2, 512])
        psM = ps("psM", [128, FREE, 512])

        const_in = sem("const_in")
        cleared = sem("cleared")
        mask_in = sem("mask_in")
        mask_step = sem("mask_step")
        mask_cols = sem("mask_cols")
        mask_ready = sem("mask_ready")
        x_in = sem("x_in")
        h_inner = sem("h_inner")
        h_made = sem("h_made")
        l_inner = sem("l_inner")
        l_made = sem("l_made")
        f_in = sem("f_in")
        box_step = sem("box_step")
        norm_cols = sem("norm_cols")
        r_step = sem("r_step")
        root_made = sem("root_made")
        r_psum = sem("r_psum")
        r_rows = sem("r_rows")
        blk_psum = sem("blk_psum")
        blk_h = sem("blk_h")
        blk_l = sem("blk_l")
        g_ready = sem("g_ready")
        g_read = sem("g_read")
        max_made = sem("max_made")
        dve_gate = sem("dve_gate")
        pe_gate = sem("pe_gate")
        sp_gate = sem("sp_gate")
        pool_gate = sem("pool_gate")
        neg_made = sem("neg_made")
        s_read = sem("s_read")
        lse_dve = sem("lse_dve")
        lse_act = sem("lse_act")
        lse_psum = sem("lse_psum")
        lse_rows = sem("lse_rows")
        lse_wrap = sem("lse_wrap")
        arg_made = sem("arg_made")
        y_made = sem("y_made")
        sh_in = [sem(f"sh_in{i}") for i in range(FREE)]
        shj_in = sem("shj_in")
        y1_made = sem("y1_made")
        z_made = sem("z_made")
        zh_made = sem("zh_made")
        zl_made = sem("zl_made")
        z_used = sem("z_used")
        o_read = sem("o_read")
        stored = sem("stored")

        NB = NK * TILES
        GROUPS = 4
        PAIRS = TILES // 2
        CLEARED = 11
        BOX_STEPS = 8
        R_STEPS = 6
        LSE_STEPS = 6

        def cols(k, stored_too=True):
            s0, n, w = CHUNKS[k]
            return (s0 + 1) * TW, (w if stored_too else n) * TW

        def out_parts(k):
            s0, _, w = CHUNKS[k]
            for j in range(STRIPS):
                q = [TILES * j + s for s in range(s0, s0 + w) if s > 0 or j == 0]
                for a in range(2):
                    rows = [r for r in q if 1 - a <= r <= HALF - a]
                    if rows:
                        yield a, j, rows[0] - TILES * j - s0, len(rows), rows[0] - 1 + a

        N_OUT = [len(list(out_parts(k))) for k in range(NK)]
        N_X = 6
        N_F = 6

        block = ctx.enter_context(nc.Block())

        @block.sync
        def _(sp):
            sp.dma_start(idn[:, :], ident).then_inc(const_in, 16)
            sp.dma_start(vld[:, :], valid).then_inc(const_in, 16)
            for layer, m in enumerate((mask0, mask1)):
                sp.dma_start(G[layer:layer + 1, 0:SIDE * SIDE],
                             m.rearrange("o c h w -> (o c) (h w)")).then_inc(mask_in, 16)

            def load_image(src):
                for a in range(2):
                    rows = src.rearrange("c (h two) w -> two c h w", two=2)[1 - a]
                    v = XP[64 * a:64 * a + 64, :, :].rearrange("p (t j) w -> p j t w", j=STRIPS)
                    for j in range(STRIPS):
                        lo, hi = max(TILES * j, 1 - a), min(TILES * (j + 1), HALF + 1 - a)
                        h = lo - 1 + a
                        sp.dma_start(v[:, j, lo - TILES * j:hi - TILES * j, 1:1 + SIDE],
                                     rows[:, h:h + hi - lo, :]).then_inc(x_in, 16)

            def lay_out_features(u):
                sp.wait_ge(h_made, 2 * (u + 1))
                sp.wait_ge(l_made, 2 * (u + 1))
                up, n = slice(64, 128), FLEN
                for dst, src in ((HL[0:64, :], LH[up, :]), (LH[0:64, :], HL[up, :]),
                                 (H1[0:64, :], LH[up, :]), (H1[up, 0:n - 1], LH[up, 1:n]),
                                 (HV[0:64, :], LH[up, :]), (HV[up, 0:n - TW], LH[up, TW:n])):
                    sp.dma_start(dst, src).then_inc(f_in, 16)

            def store_chunk(u, k, dst):
                sp.wait_ge(o_read, (u * NK + k + 1) * 2 + 2 * FREE)
                v = OSB[:, :, :].rearrange("p (s j) w -> p j s w", j=STRIPS)
                for a, j, s, n, h in out_parts(k):
                    rows = dst.rearrange("c (h two) w -> two c h w", two=2)[1 - a]
                    sp.dma_start(rows[:, h:h + n, :],
                                 v[64 * a:64 * a + 64, j, s:s + n, 1:1 + SIDE]).then_inc(stored, 16)

            def shift(u, k, t, par):
                c0, n = cols(k)
                i = (u * NK + k) * TILES + t
                sp.wait_ge(y_made, i + 1)
                sp.wait_ge(y1_made, i + 1)
                sp.dma_start(SH[1:TW, par, 1:n], G[0:TW - 1, bass.ds(t * GLEN + c0, n - 1)]).then_inc(sh_in[par], 16)

            def shift_strip(u, k):
                c0, n = cols(k)
                c = u * NK + k
                sp.wait_ge(y1_made, (c + 1) * TILES + FREE)
                sp.sem_inc(sp_gate, 1)
                sp.wait_ge(z_made, c * TILES + 1)
                above = (TILES - 1) * GLEN + c0 - TW
                sp.dma_start(SHJ[PITCH:TW, 0:n], G[0:TW - PITCH, above:above + n]).then_inc(shj_in, 16)

            def unit(u, following, dst):
                if following is not None:
                    sp.wait_ge(h_inner, u + 1)
                    sp.wait_ge(l_inner, u + 1)
                    sp.wait_ge(box_step, u * BOX_STEPS + 2)
                    sp.sem_inc(sp_gate, 1)
                    sp.wait_ge(blk_psum, (u + 1) * PAIRS)
                    sp.wait_ge(stored, u * sum(N_OUT) * 16 + 16)
                    load_image(following)
                    lay_out_features(u + 1)
                for k in range(NK):
                    with sp.Fori(0, PAIRS) as i:
                        for par in range(FREE):
                            shift(u, k, 2 * i + par, par)
                    if k >= 1:
                        store_chunk(u, k - 1, dst)
                    shift_strip(u, k)
                store_chunk(u, NK - 1, dst)

            sp.sem_inc(stored, 16)
            sp.wait_ge(cleared, CLEARED)
            load_image(x[0])
            lay_out_features(0)
            for layer in range(LAYERS):
                src, dst = (x, mid) if layer == 0 else (mid, out)
                with sp.Fori(0, IMAGES - 1) as b:
                    unit(layer * IMAGES + b, src[bass.ds(b + 1, 1)].rearrange("o c h w -> (o c) h w"),
                         dst[bass.ds(b, 1)].rearrange("o c h w -> (o c) h w"))
                unit((layer + 1) * IMAGES - 1, mid[0] if layer + 1 < LAYERS else None, dst[IMAGES - 1])
            sp.wait_ge(stored, (UNITS * sum(N_OUT) + 1) * 16)

        @block.tensor
        def _(pe):
            pe.sem_inc(z_used, FREE)
            pe.wait_ge(const_in, 32)
            pe.wait_ge(cleared, CLEARED)
            pe.wait_ge(mask_step, 6)
            for t in range(TILES):
                last = pe.matmul(psM[0:TW, 0, 2 * t:2 * t + 2], SQ[0:LAYERS, t * TW:(t + 1) * TW],
                                 idn[0:LAYERS, 0:LAYERS], start=True, stop=True)
            last.then_inc(mask_cols, 1)
            pe.wait_ge(mask_ready, 1)

            def norms(u):
                pe.wait_ge(box_step, (u + 1) * BOX_STEPS)
                pe.wait_ge(lse_rows, u * GROUPS + 1)
                for t in range(TILES):
                    last = pe.matmul(psM[0:TW, 0, t:t + 1], SQ[64:128, t * TW:(t + 1) * TW], ones[64:128, :],
                                     start=True, stop=True)
                last.then_inc(norm_cols, 1)

            def spread(u, col, made, read, start=0):
                for g in range(GROUPS):
                    if g >= 2:
                        pe.wait_ge(read, u * GROUPS + g - 1 + start)
                    for t in range(4 * g, min(4 * g + 4, TILES)):
                        last = pe.matmul(psM[0:TW, g % 2, (t % 4) * TW:(t % 4 + 1) * TW],
                                         col[:, t:t + 1].to_broadcast([TW, TW]), idn[0:TW, 0:TW],
                                         start=True, stop=True)
                    last.then_inc(made, 1)

            def blocks(u):
                for g in range(PAIRS):
                    if g == 0:
                        pe.wait_ge(r_rows, (u + 1) * GROUPS)
                    if g >= 2:
                        pe.wait_ge(blk_l, u * PAIRS + g - 1)
                    for t in (2 * g, 2 * g + 1):
                        for b in range(2):
                            xt = XP[:, t * STRIPS:(t + 1) * STRIPS, :].rearrange("p r w -> p (r w)")[:, b:2 * TW:2]
                            o = (t % 2 * 2 + b) * 128
                            last = pe.transpose(psM[0:TW, g % 2, o:o + 128], xt, idn[:, :])
                    last.then_inc(blk_psum, 1)

            TERMS = [(HL, LH, dy, dx) for dy in range(3) for dx in range(3)]
            TERMS += [(H1, H1, dy, 0) for dy in range(3)]
            TERMS += [(HV, HV, 0, 2), (HL, HL, 2, 2)]

            def score_tile(u, k, t, par):
                s0, _, w = CHUNKS[k]
                n = w * TW
                pe.wait_ge(g_read, (u * NK + k) * TILES + t + 1)
                for i, (st, mv, dy, dx) in enumerate(TERMS):
                    lo = (s0 + dy) * TW + dx
                    last = pe.matmul(psG[0:TW, par, 0:n], st[:, bass.ds((t + dy) * TW + dx, TW)], mv[:, lo:lo + n],
                                     start=(i == 0), stop=(i == len(TERMS) - 1))
                last.then_inc(g_ready, 1)

            def paste_tile(u, k, t, par, order, first=False, end=False):
                n = cols(k)[1]
                z = (u * NK + k) * TILES + order
                pe.wait_ge(zh_made, z + 1 + FREE)
                pe.wait_ge(zl_made, z + 1 + FREE)
                for b in range(2):
                    for i, (w, m) in enumerate(((Bh, Zh), (Bl, Zh), (Bh, Zl))):
                        last = pe.matmul(psO[:, k % 2, b, 0:n],
                                         w[:, bass.ds((2 * t + b) * 128, 128)], m[:, par, 0:n],
                                         start=first and i == 0, stop=end and i == 2)
                last.then_inc(z_used, 1)

            with pe.Fori(0, UNITS) as u:
                norms(u)
                pe.wait_ge(r_step, (u + 1) * R_STEPS)
                spread(u, R, r_psum, r_rows)
                blocks(u)
                pe.wait_ge(f_in, (u + 1) * N_F * 16)
                pe.sem_inc(pe_gate, 1)
                for k in range(NK):
                    with pe.Fori(0, PAIRS) as i:
                        for par in range(FREE):
                            score_tile(u, k, 2 * i + par, par)
                pe.wait_ge(lse_dve, (u + 1) * LSE_STEPS)
                pe.wait_ge(blk_l, (u + 1) * PAIRS)
                spread(u, lse, lse_psum, lse_rows, 1)
                for k in range(NK):
                    pe.wait_ge(o_read, (u * NK + k + 1) * 2)
                    paste_tile(u, k, 1, 1, 0, first=True)
                    paste_tile(u, k, 2, 0, 1)
                    with pe.Fori(1, PAIRS - 1) as i:
                        paste_tile(u, k, 2 * i + 1, 1, 2 * i)
                        paste_tile(u, k, 2 * i + 2, 0, 2 * i + 1)
                    paste_tile(u, k, TILES - 1, 1, TILES - 2)
                    paste_tile(u, k, 0, 0, TILES - 1, end=True)

        @block.scalar
        def _(act):
            act.sem_inc(g_read, FREE)
            act.sem_inc(s_read, FREE)
            act.sem_inc(zh_made, FREE)
            act.sem_inc(o_read, 2 * FREE)
            act.sem_inc(lse_rows, 1)

            def high_features(u):
                act.wait_ge(x_in, (u + 1) * N_X * 16)
                if not (isinstance(u, int) and u == 0):
                    act.wait_ge(f_in, u * N_F * 16)
                    act.wait_ge(g_ready, u * NB)
                act.activation(LH[64:128, TW:TW * (TILES + 1)].rearrange("p (r w) -> p r w", w=PITCH)[:, :, 1:1 + HALF],
                               XP[64:128, :, 1:1 + SIDE:2], ACT.Copy).then_inc(h_inner, 1)
                act.wait_ge(h_inner, u + 1)
                act.activation(LH[64:128, PITCH:TW], LH[64:128, TILES * TW:TILES * TW + 2 * PITCH],
                               ACT.Copy).then_inc(h_made, 1)
                act.activation(LH[64:128, (TILES + 1) * TW:(TILES + 3) * TW].rearrange("p (r w) -> p r w", w=TW)[:, :, 0:2 * PITCH],
                               LH[64:128, TW:3 * TW].rearrange("p (r w) -> p r w", w=TW)[:, :, PITCH:TW],
                               ACT.Copy).then_inc(h_made, 1)

            def read_rows(u, made, read):
                for g in range(GROUPS):
                    act.wait_ge(made, u * GROUPS + g + 1)
                    n = min(4, TILES - 4 * g) * TW
                    act.activation(BC[:, 4 * g * TW:4 * g * TW + n], psM[0:TW, g % 2, 0:n], ACT.Copy).then_inc(read, 1)

            def high_blocks(u):
                act.wait_ge(z_used, u * NB + FREE)
                for g in range(PAIRS):
                    act.wait_ge(blk_psum, u * PAIRS + g + 1)
                    act.activation(Bh[:, g * 512:(g + 1) * 512], psM[0:TW, g % 2, :], ACT.Copy).then_inc(blk_h, 1)

            def score_tile(u, k, t, par):
                c0, n = cols(k)
                i = (u * NK + k) * TILES + t
                act.wait_ge(max_made, i + 1)
                act.activation(G[:, bass.ds(t * GLEN + c0, n)], psG[0:TW, par, 0:n], ACT.Copy).then_inc(g_read, 1)
                act.wait_ge(neg_made, i + 1)
                v = S[:, par, :].rearrange("p (s w) -> p s w", w=PITCH)
                parts = [v[:, 0:STRIPS * CHUNKS[k][1], 0:HALF]]
                if k == NK - 1:
                    parts = [v[:, 0:5, 0:HALF], v[:, 6:8, 0:HALF]]
                for j, e in enumerate(parts):
                    last = act.activation(e, e, ACT.Exp, bias=nm[:, bass.ds(k * TILES + t, 1)],
                                          accum_out=sg[:, bass.ds((k + j) * TILES + t, 1)])
                last.then_inc(s_read, 1)

            def softmax_tile(u, k, t):
                c0, n = cols(k)
                i = (u * NK + k) * TILES + t
                act.wait_ge(arg_made, i + 2)
                y = G[:, bass.ds(t * GLEN + c0, n)]
                act.activation(y, y, ACT.Exp, bias=nb[:, bass.ds(u * TILES + t, 1)]).then_inc(y_made, 1)

            def high_z(u, k, par, order):
                z = (u * NK + k) * TILES + order
                n = cols(k)[1]
                act.wait_ge(z_made, z + 2)
                act.wait_ge(z_used, z + 1)
                act.activation(Zh[:, par, 0:n], Z[:, par, 0:n], ACT.Copy, scale=ZSCALE).then_inc(zh_made, 1)

            def read_out(u, k):
                c = u * NK + k
                n = cols(k)[1]
                act.wait_ge(z_used, (c + 1) * TILES + FREE)
                act.wait_ge(stored, (u * sum(N_OUT) + sum(N_OUT[:k]) + 1) * 16)
                for b in range(2):
                    act.activation(OSB[:, 0:n // PITCH, b:b + 2 * HALF + 1:2],
                                   psO[:, k % 2, b, 0:n].rearrange("p (s w) -> p s w", w=PITCH)[:, :, 0:HALF + 1],
                                   ACT.Copy, scale=0.25 / ZSCALE).then_inc(o_read, 1)

            def unit(u, more):
                act.wait_ge(r_step, u * R_STEPS + 1)
                act.activation(root[:, :], nsq[:, :], ACT.Sqrt).then_inc(root_made, 1)
                act.wait_ge(arg_made, u * NB + 1)
                read_rows(u, r_psum, r_rows)
                high_blocks(u)
                act.wait_ge(z_made, u * NB + 1)
                for k in range(NK):
                    with act.Fori(0, PAIRS) as i:
                        for par in range(FREE):
                            score_tile(u, k, 2 * i + par, par)
                act.wait_ge(lse_dve, u * LSE_STEPS + 2)
                act.activation(ed[:, :], df[:, :], ACT.Exp).then_inc(lse_act, 1)
                act.wait_ge(lse_dve, u * LSE_STEPS + 4)
                act.activation(lns[:, :], tot[:, :], ACT.Ln).then_inc(lse_act, 1)
                read_rows(u, lse_psum, lse_rows)
                act.wait_ge(lse_rows, (u + 1) * GROUPS + 1)
                act.activation(BC[:, TILES * TW:TILES * TW + 2 * PITCH], BC[:, PITCH:TW], ACT.Copy).then_inc(lse_wrap, 1)
                if more:
                    high_features(u + 1)
                for k in range(NK + 1):
                    with act.Fori(0, PAIRS) as i:
                        if k >= 1:
                            high_z(u, k - 1, 1, 2 * i)
                            high_z(u, k - 1, 0, 2 * i + 1)
                        if k < NK:
                            softmax_tile(u, k, 2 * i)
                            softmax_tile(u, k, 2 * i + 1)
                    if k >= 1:
                        read_out(u, k - 1)

            act.wait_ge(cleared, CLEARED)
            high_features(0)
            with act.Fori(0, UNITS - 1) as u:
                unit(u, True)
            unit(UNITS - 1, False)

        def box_sums(eng, p0, p1, step, base):
            wide, tall = (TILES + 2) * TW, TILES * TW
            sq, bx = SQ[p0:p1, :], BX[p0:p1, :]
            eng.tensor_tensor(bx[:, 0:wide], sq[:, 0:wide], sq[:, 1:wide + 1], ALU.add).then_inc(step, 1)
            eng.wait_ge(step, base + 1)
            eng.tensor_tensor(bx[:, 0:wide], bx[:, 0:wide], sq[:, 2:wide + 2], ALU.add).then_inc(step, 1)
            eng.wait_ge(step, base + 2)
            eng.tensor_tensor(sq[:, 0:tall], bx[:, 0:tall], bx[:, TW:TW + tall], ALU.add).then_inc(step, 1)
            eng.wait_ge(step, base + 3)
            eng.tensor_tensor(sq[:, 0:tall], sq[:, 0:tall], bx[:, 2 * TW:2 * TW + tall], ALU.add).then_inc(step, 1)

        @block.vector
        def _(dve):
            for tile, value in ((XP[:, :, :], 0.0), (HL[:, :].bitcast(F32), 0.0), (LH[:, :].bitcast(F32), 0.0),
                                (H1[:, :].bitcast(F32), 0.0), (HV[:, :].bitcast(F32), 0.0), (ones[:, :], 1.0),
                                (SH[:, :, :], 0.0), (SHJ[:, :], 0.0),
                                (BC[:, TILES * TW:SLOTS * TW], BIG)):
                dve.memset(tile, value).then_inc(cleared, 1)
            dve.sem_inc(zl_made, FREE)
            dve.sem_inc(arg_made, 1)
            dve.sem_inc(z_made, 1)
            dve.memset(SQ[0:LAYERS, :], 0.0).then_inc(mask_step, 1)
            dve.wait_ge(mask_in, 32)
            dve.wait_ge(mask_step, 1)
            m = G[0:LAYERS, 0:SIDE * SIDE].rearrange("p (h w) -> p h w", w=SIDE)
            f = SQ[0:LAYERS, 0:FROWS * TW].rearrange("p (r j w) -> p j r w", j=STRIPS, w=PITCH)
            for j in range(STRIPS):
                lo, hi = max(TILES * j - 1, 0), min(TILES * j + TILES + 2, HALF)
                r = lo - (TILES * j - 1)
                last = dve.tensor_copy(f[:, j, r:r + hi - lo, 1:1 + HALF], m[:, 2 * lo:2 * hi:2, 0:SIDE:2])
            last.then_inc(mask_step, 1)
            dve.wait_ge(mask_step, 2)
            box_sums(dve, 0, LAYERS, mask_step, 2)
            dve.memset(G[:, :].rearrange("p (t c) -> p t c", c=GLEN)[:, :, 0:TW], 0.0)
            dve.wait_ge(mask_cols, 1)
            dve.wait_ge(const_in, 32)
            dve.tensor_scalar(mmc[:, :, :], psM[0:TW, 0, 0:LAYERS * TILES].rearrange("p (t l) -> p l t", l=LAYERS),
                              0.0, None, ALU.is_equal).then_inc(mask_ready, 1)
            dve.wait_ge(mask_ready, 1)
            for layer in range(LAYERS):
                last = dve.tensor_tensor(mmc[:, layer, :], mmc[:, layer, :], vld[:, :], ALU.mult)
            last.then_inc(mask_ready, 1)
            dve.wait_ge(mask_ready, 2)
            for u in range(UNITS):
                at = slice(u * TILES, (u + 1) * TILES)
                dve.tensor_scalar(mm20[:, at], mmc[:, u // IMAGES, :], 20.0, None, ALU.mult).then_inc(mask_ready, 1)
                dve.tensor_scalar(nb[:, at], mmc[:, u // IMAGES, :], -1.0, BIG, ALU.add, ALU.mult).then_inc(mask_ready, 1)
            dve.tensor_scalar(big[:, :], vld[:, :], -2.0 * BIG, BIG, ALU.mult, ALU.add).then_inc(mask_ready, 1)
            dve.wait_ge(mask_ready, 2 + 2 * UNITS + 1)

            def low_features(u):
                dve.wait_ge(h_inner, u + 1)
                inner = lambda a: a[64:128, TW:TW * (TILES + 1)].rearrange("p (r w) -> p r w", w=PITCH)[:, :, 1:1 + HALF]
                dve.tensor_tensor(inner(HL), XP[64:128, :, 1:1 + SIDE:2], inner(LH), ALU.subtract).then_inc(l_inner, 1)
                dve.wait_ge(l_inner, u + 1)
                dve.tensor_copy(HL[64:128, PITCH:TW], HL[64:128, TILES * TW:TILES * TW + 2 * PITCH]).then_inc(l_made, 1)
                dve.tensor_copy(HL[64:128, (TILES + 1) * TW:(TILES + 3) * TW].rearrange("p (r w) -> p r w", w=TW)[:, :, 0:2 * PITCH],
                                HL[64:128, TW:3 * TW].rearrange("p (r w) -> p r w", w=TW)[:, :, PITCH:TW]).then_inc(l_made, 1)

            def scales(u):
                dve.wait_ge(norm_cols, u + 1)
                at = u * R_STEPS
                dve.tensor_scalar(nsq[:, :], psM[0:TW, 0, 0:TILES], 1e-8, None, ALU.max).then_inc(r_step, 1)
                dve.wait_ge(root_made, u + 1)
                dve.reciprocal(rcp[:, :], root[:, :]).then_inc(r_step, 1)
                dve.wait_ge(r_step, at + 2)
                dve.tensor_tensor(quo[:, :], nsq[:, :], rcp[:, :], ALU.mult).then_inc(r_step, 1)
                dve.wait_ge(r_step, at + 3)
                dve.tensor_tensor(nrm2[:, :], quo[:, :], root[:, :], ALU.add).then_inc(r_step, 1)
                dve.wait_ge(r_step, at + 4)
                dve.reciprocal(rcp[:, :], nrm2[:, :]).then_inc(r_step, 1)
                dve.wait_ge(r_step, at + 5)
                dve.tensor_tensor(R[:, :], rcp[:, :], mm20[:, bass.ds(u * TILES, TILES)], ALU.mult).then_inc(r_step, 1)

            def low_blocks(u):
                for g in range(PAIRS):
                    dve.wait_ge(blk_h, u * PAIRS + g + 1)
                    at = slice(g * 512, (g + 1) * 512)
                    dve.tensor_tensor(Bl[:, at], psM[0:TW, g % 2, :], Bh[:, at], ALU.subtract).then_inc(blk_l, 1)

            def score_tile(u, k, t, par):
                s0, w, _ = CHUNKS[k]
                n = w * TW
                i = (u * NK + k) * TILES + t
                dve.wait_ge(g_ready, i + 1)
                dve.wait_ge(s_read, i + 1)
                dve.sem_inc(dve_gate, 1)
                dve.tensor_tensor_reduce(S[:, par, 0:n], psG[0:TW, par, 0:n], BC[:, s0 * TW:s0 * TW + n], 1.0, 0.0,
                                         ALU.mult, ALU.max, mx[:, par:par + 1]).then_inc(max_made, 1)
                dve.wait_ge(max_made, i + 1)
                dve.tensor_scalar(nm[:, bass.ds(k * TILES + t, 1)], mx[:, par:par + 1], -1.0, None,
                                  ALU.mult).then_inc(neg_made, 1)

            def log_sums(u):
                at = u * LSE_STEPS
                by_tile = lambda a: a.rearrange("p (k t) -> p t k", t=TILES)
                dve.wait_ge(s_read, (u + 1) * NB + FREE)
                last = slice((NK - 1) * TILES, NK * TILES)
                dve.tensor_reduce(nM[:, :], by_tile(nm[:, :]), AX.X, ALU.min).then_inc(lse_dve, 1)
                dve.tensor_tensor(sg[:, last], sg[:, last], sg[:, NK * TILES:], ALU.add)
                dve.wait_ge(lse_dve, at + 1)
                dve.tensor_tensor(df[:, :].rearrange("p (k t) -> p k t", t=TILES),
                                  nM[:, :].unsqueeze(1).to_broadcast([TW, NK, TILES]),
                                  nm[:, :].rearrange("p (k t) -> p k t", t=TILES), ALU.subtract).then_inc(lse_dve, 1)
                dve.wait_ge(lse_act, u * 2 + 1)
                dve.tensor_tensor(df[:, :], ed[:, :], sg[:, 0:NK * TILES], ALU.mult).then_inc(lse_dve, 1)
                dve.wait_ge(lse_dve, at + 3)
                dve.tensor_reduce(tot[:, :], by_tile(df[:, :]), AX.X, ALU.add).then_inc(lse_dve, 1)
                dve.wait_ge(lse_act, u * 2 + 2)
                dve.tensor_tensor(tot[:, :], lns[:, :], nM[:, :], ALU.subtract).then_inc(lse_dve, 1)
                dve.wait_ge(lse_dve, at + 5)
                dve.tensor_tensor(lse[:, :], tot[:, :], big[:, :], ALU.max).then_inc(lse_dve, 1)

            def argument(u, k, t):
                s0, _, w = CHUNKS[k]
                c0, n = cols(k)
                g = G[:, bass.ds(t * GLEN + c0, n)]
                dve.scalar_tensor_tensor(out=g, in0=g, scalar=R[:, bass.ds(t, 1)], in1=BC[:, s0 * TW:s0 * TW + n],
                                         op0=ALU.mult, op1=ALU.subtract).then_inc(arg_made, 1)

            def sum_z(u, k, t, par, order):
                c0, n = cols(k)
                c = u * NK + k
                if isinstance(t, int) and t == 0:
                    dve.wait_ge(shj_in, (c + 1) * 16)
                    above = SHJ[:, 0:n]
                else:
                    dve.wait_ge(y1_made, c * TILES + t + 1 + FREE)
                    above = G[:, bass.ds((t - 1) * GLEN + c0 - TW, n)]
                dve.wait_ge(zh_made, c * TILES + order + 1)
                dve.wait_ge(zl_made, c * TILES + order + 1)
                dve.tensor_tensor(Z[:, par, 0:n], G[:, bass.ds(t * GLEN + c0, n)], above, ALU.add).then_inc(z_made, 1)

            def low_z(u, k, par, order):
                n = cols(k)[1]
                dve.wait_ge(zh_made, (u * NK + k) * TILES + order + 1 + FREE)
                dve.scalar_tensor_tensor(out=Zl[:, par, 0:n], in0=Z[:, par, 0:n], scalar=ZSCALE, in1=Zh[:, par, 0:n],
                                         op0=ALU.mult, op1=ALU.subtract).then_inc(zl_made, 1)

            def unit(u, more):
                scales(u)
                low_blocks(u)
                dve.wait_ge(r_rows, (u + 1) * GROUPS)
                dve.sem_inc(dve_gate, 1)
                for k in range(NK):
                    with dve.Fori(0, PAIRS) as i:
                        for par in range(FREE):
                            score_tile(u, k, 2 * i + par, par)
                log_sums(u)
                if more:
                    low_features(u + 1)
                dve.wait_ge(lse_wrap, u + 1)
                dve.sem_inc(dve_gate, 1)

                def step(k, i, last):
                    if k >= 1:
                        sum_z(u, k - 1, 2 * i + 1, 1, 2 * i)
                        sum_z(u, k - 1, 0 if last else 2 * i + 2, 0, 2 * i + 1)
                    if k < NK:
                        argument(u, k, 2 * i)
                        argument(u, k, 2 * i + 1)
                    if k >= 1:
                        low_z(u, k - 1, 1, 2 * i)
                        low_z(u, k - 1, 0, 2 * i + 1)

                for k in range(NK + 1):
                    with dve.Fori(0, PAIRS - 1) as i:
                        step(k, i, False)
                    step(k, PAIRS - 1, True)

            low_features(0)
            with dve.Fori(0, UNITS - 1) as u:
                unit(u, True)
            unit(UNITS - 1, False)

        @block.gpsimd
        def _(pool):
            for tile in (SQ[64:128, :], BX[64:128, :]):
                pool.memset(tile, 0.0).then_inc(cleared, 1)
            pool.sem_inc(y1_made, FREE)

            def squares(u):
                at = u * BOX_STEPS
                if not (isinstance(u, int) and u == 0):
                    pool.wait_ge(norm_cols, u)
                pool.wait_ge(x_in, (u + 1) * N_X * 16)
                pool.sem_inc(pool_gate, 1)
                pool.memset(SQ[64:128, :], 0.0).then_inc(box_step, 1)
                pool.wait_ge(box_step, at + 1)
                f = XP[64:128, :, 1:1 + SIDE:2]
                pool.tensor_tensor(SQ[64:128, TW:TW * (TILES + 1)].rearrange("p (r w) -> p r w", w=PITCH)[:, :, 1:1 + HALF],
                                   f, f, ALU.mult).then_inc(box_step, 1)
                pool.wait_ge(box_step, at + 2)
                pool.sem_inc(pool_gate, 1)
                pool.tensor_copy(SQ[64:128, PITCH:TW], SQ[64:128, TILES * TW:TILES * TW + 2 * PITCH]).then_inc(box_step, 1)
                pool.tensor_copy(SQ[64:128, (TILES + 1) * TW:(TILES + 3) * TW].rearrange("p (r w) -> p r w", w=TW)[:, :, 0:2 * PITCH],
                                 SQ[64:128, TW:3 * TW].rearrange("p (r w) -> p r w", w=TW)[:, :, PITCH:TW]).then_inc(box_step, 1)
                pool.wait_ge(box_step, at + 4)
                box_sums(pool, 64, 128, box_step, at + 4)

            def sum_y1(u, k, t, par, i):
                c0, n = cols(k)
                pool.wait_ge(sh_in[par], ((u * NK + k) * PAIRS + i + 1) * 16)
                g = G[:, bass.ds(t * GLEN + c0, n)]
                pool.tensor_tensor(g, g, SH[:, par, 0:n], ALU.add).then_inc(y1_made, 1)

            def unit(u, more):
                if more:
                    pool.wait_ge(y1_made, u * NB + FREE)
                    squares(u + 1)
                    pool.wait_ge(box_step, (u + 2) * BOX_STEPS)
                    pool.sem_inc(pool_gate, 1)
                for k in range(NK):
                    with pool.Fori(0, PAIRS) as i:
                        for par in range(FREE):
                            sum_y1(u, k, 2 * i + par, par, i)

            pool.wait_ge(cleared, CLEARED)
            squares(0)
            with pool.Fori(0, UNITS - 1) as u:
                unit(u, True)
            unit(UNITS - 1, False)


def kernel(x, L0_conv_mask, L1_conv_mask):
    import numpy as np
    import concourse.bacc as bacc
    from concourse.bass_utils import run_bass_kernel_spmd

    nc = bacc.Bacc("TRN2", target_bir_lowering=False, num_devices=1)
    rows = np.arange(TW) // PITCH * TILES
    valid = (rows[:, None] + np.arange(TILES)[None, :] < HALF) & (np.arange(TW) % PITCH < HALF)[:, None]
    arrays = {
        "x": np.ascontiguousarray(x),
        "mask0": np.ascontiguousarray(L0_conv_mask),
        "mask1": np.ascontiguousarray(L1_conv_mask),
        "ident": np.eye(128, dtype=np.float32),
        "valid": valid.astype(np.float32),
    }
    ins = [nc.dram_tensor(n, a.shape, mybir.dt.from_np(a.dtype), kind="ExternalInput").ap() for n, a in arrays.items()]
    out = nc.dram_tensor("out", (IMAGES, C, SIDE, SIDE), F32, kind="ExternalOutput").ap()
    contextual_attention(nc, *ins, out)
    return run_bass_kernel_spmd(nc, [arrays], core_ids=[0]).results[0]["out"]
```

```python
from contextlib import ExitStack

import concourse.bass as bass
from concourse import mybir

F32 = mybir.dt.float32
F16 = mybir.dt.float16
ALU = mybir.AluOpType
ACT = mybir.ActivationFunctionType
AX = mybir.AxisListType

LAYERS, IMAGES, C, SIDE = 2, 4, 64, 80
UNITS = LAYERS * IMAGES
HALF = SIDE // 2
STRIPS, TILES = 3, 14
PITCH = HALF + 2
TW = STRIPS * PITCH
FROWS = TILES + 2
FLEN = FROWS * TW + 4
WRAP = 2 * PITCH
CLEN = TILES * TW + WRAP
GLEN = TW + CLEN
CHUNKS = [(0, 4), (4, 4), (8, 3), (11, 3)]
NK = len(CHUNKS)
ZSCALE = 4096.0
BIG = 1.0e30
FREE = 2
EXP_AND_LN = 6


def contextual_attention(nc, x, mask0, mask1, ident, valid, out):
    mid = nc.dram_tensor("mid", (IMAGES, C, SIDE, SIDE), F32, kind="Internal").ap()

    with ExitStack() as ctx:
        def sb(name, shape, dt):
            return ctx.enter_context(nc.sbuf_tensor(name, shape, dt))

        def ps(name, shape):
            return ctx.enter_context(nc.psum_tensor(name, shape, F32))

        def sem(name):
            return ctx.enter_context(nc.semaphore(name))

        G = sb("G", [TW, TILES * GLEN], F32)
        HL = sb("HL", [128, FLEN], F16)
        LH = sb("LH", [128, FLEN], F16)
        H1 = sb("H1", [128, FLEN], F16)
        HV = sb("HV", [128, FLEN], F16)
        XP = sb("XP", [128, TILES * STRIPS, 2 * PITCH], F32)
        Bh = sb("Bh", [TW, TILES * 2 * 128], F16)
        Bl = sb("Bl", [TW, TILES * 2 * 128], F16)
        SQ = sb("SQ", [128, FLEN], F32)
        BX = sb("BX", [128, FLEN], F32)
        RB = sb("RB", [TW, TILES * TW], F32)
        BC = sb("BC", [TW, CLEN], F32)
        S = sb("S", [TW, FREE, 4 * TW], F32)
        SH = sb("SH", [TW, FREE, 4 * TW], F32)
        SHJ = sb("SHJ", [TW, 4 * TW], F32)
        Z = sb("Z", [TW, FREE, 4 * TW], F32)
        Zh = sb("Zh", [TW, FREE, 4 * TW], F16)
        Zl = sb("Zl", [TW, FREE, 4 * TW], F16)
        OSB = sb("OSB", [128, 4 * STRIPS, 2 * PITCH], F32)
        idn = sb("idn", [128, 128], F32)
        ones = sb("ones", [128, 1], F32)
        vld = sb("vld", [TW, TILES], F32)
        big = sb("big", [TW, TILES], F32)
        mm20 = sb("mm20", [TW, UNITS * TILES], F32)
        nb = sb("nb", [TW, UNITS * TILES], F32)
        mmc = sb("mmc", [TW, LAYERS, TILES], F32)
        nsq = sb("nsq", [TW, TILES], F32)
        root = sb("root", [TW, TILES], F32)
        lnn = sb("lnn", [TW, TILES], F32)
        quo = sb("quo", [TW, TILES], F32)
        nrm2 = sb("nrm2", [TW, TILES], F32)
        rcp = sb("rcp", [TW, TILES], F32)
        R = sb("R", [TW, TILES], F32)
        RA = sb("RA", [TW, UNITS * TILES], F32)
        mx = sb("mx", [TW, FREE], F32)
        nm = sb("nm", [TW, NK * TILES], F32)
        sg = sb("sg", [TW, (NK + 1) * TILES], F32)
        nM = sb("nM", [TW, TILES], F32)
        df = sb("df", [TW, NK * TILES], F32)
        ed = sb("ed", [TW, NK * TILES], F32)
        tot = sb("tot", [TW, TILES], F32)
        lns = sb("lns", [TW, TILES], F32)
        lse = sb("lse", [TW, TILES], F32)

        psG = ps("psG", [128, FREE, 512])
        psO = ps("psO", [128, FREE, 2, 512])
        psM = ps("psM", [128, FREE, 512])

        const_in = sem("const_in")
        cleared = sem("cleared")
        mask_in = sem("mask_in")
        mask_step = sem("mask_step")
        mask_cols = sem("mask_cols")
        mask_ready = sem("mask_ready")
        x_in = sem("x_in")
        h_inner = sem("h_inner")
        h_made = sem("h_made")
        l_inner = sem("l_inner")
        l_made = sem("l_made")
        f_in = sem("f_in")
        box_step = sem("box_step")
        norm_cols = sem("norm_cols")
        r_step = sem("r_step")
        root_made = sem("root_made")
        r_psum = sem("r_psum")
        r_rows = sem("r_rows")
        blk_psum = sem("blk_psum")
        blk_h = sem("blk_h")
        blk_l = sem("blk_l")
        g_ready = sem("g_ready")
        g_read = sem("g_read")
        max_made = sem("max_made")
        dve_gate = sem("dve_gate")
        pe_gate = sem("pe_gate")
        sp_gate = sem("sp_gate")
        pool_gate = sem("pool_gate")
        neg_made = sem("neg_made")
        s_read = sem("s_read")
        lse_dve = sem("lse_dve")
        lse_act = sem("lse_act")
        lse_psum = sem("lse_psum")
        lse_rows = sem("lse_rows")
        lse_wrap = sem("lse_wrap")
        arg_made = sem("arg_made")
        y_made = sem("y_made")
        sh_in = [sem(f"sh_in{i}") for i in range(FREE)]
        shj_in = sem("shj_in")
        y1_made = sem("y1_made")
        z_made = sem("z_made")
        zh_made = sem("zh_made")
        zl_made = sem("zl_made")
        z_used = sem("z_used")
        o_read = sem("o_read")
        stored = sem("stored")

        NB = NK * TILES
        GROUPS = 4
        PAIRS = TILES // 2
        CLEARED = 10
        BOX_STEPS = 8
        R_STEPS = 7
        LSE_STEPS = 6

        def cols(k, wrap=True):
            s0, n = CHUNKS[k]
            return (s0 + 1) * TW, n * TW + (WRAP if wrap and k == NK - 1 else 0)

        def out_parts(k):
            s0, n = CHUNKS[k]
            for j in range(STRIPS):
                q = [TILES * j + s for s in range(s0, s0 + n + (k == NK - 1)) if s > 0 or j == 0]
                for a in range(2):
                    rows = [r for r in q if 1 - a <= r <= HALF - a]
                    if rows:
                        yield a, j, rows[0] - TILES * j - s0, len(rows), rows[0] - 1 + a

        N_OUT = [len(list(out_parts(k))) for k in range(NK)]
        N_X = 6
        N_F = 6

        block = ctx.enter_context(nc.Block())

        @block.sync
        def _(sp):
            sp.dma_start(idn[:, :], ident).then_inc(const_in, 16)
            sp.dma_start(vld[:, :], valid).then_inc(const_in, 16)
            for layer, m in enumerate((mask0, mask1)):
                sp.dma_start(G[layer:layer + 1, 0:SIDE * SIDE],
                             m.rearrange("o c h w -> (o c) (h w)")).then_inc(mask_in, 16)

            def load_image(src):
                for a in range(2):
                    rows = src.rearrange("c (h two) w -> two c h w", two=2)[1 - a]
                    v = XP[64 * a:64 * a + 64, :, :].rearrange("p (t j) w -> p j t w", j=STRIPS)
                    for j in range(STRIPS):
                        lo, hi = max(TILES * j, 1 - a), min(TILES * (j + 1), HALF + 1 - a)
                        h = lo - 1 + a
                        sp.dma_start(v[:, j, lo - TILES * j:hi - TILES * j, 1:1 + SIDE],
                                     rows[:, h:h + hi - lo, :]).then_inc(x_in, 16)

            def lay_out_features(u):
                sp.wait_ge(h_made, 2 * (u + 1))
                sp.wait_ge(l_made, 2 * (u + 1))
                up, n = slice(64, 128), FLEN
                for dst, src in ((HL[0:64, :], LH[up, :]), (LH[0:64, :], HL[up, :]),
                                 (H1[0:64, :], LH[up, :]), (H1[up, 0:n - 1], LH[up, 1:n]),
                                 (HV[0:64, :], LH[up, :]), (HV[up, 0:n - TW], LH[up, TW:n])):
                    sp.dma_start(dst, src).then_inc(f_in, 16)

            def store_chunk(u, k, dst):
                sp.wait_ge(o_read, (u * NK + k + 1) * 2 + 2 * FREE)
                v = OSB[:, :, :].rearrange("p (s j) w -> p j s w", j=STRIPS)
                for a, j, s, n, h in out_parts(k):
                    rows = dst.rearrange("c (h two) w -> two c h w", two=2)[1 - a]
                    sp.dma_start(rows[:, h:h + n, :],
                                 v[64 * a:64 * a + 64, j, s:s + n, 1:1 + SIDE]).then_inc(stored, 16)

            def shift(u, k, t, par):
                c0, n = cols(k)
                i = (u * NK + k) * TILES + t
                sp.wait_ge(y_made, i + 1)
                sp.wait_ge(y1_made, i + 1)
                sp.dma_start(SH[1:TW, par, 1:n], G[0:TW - 1, bass.ds(t * GLEN + c0, n - 1)]).then_inc(sh_in[par], 16)

            def shift_strip(u, k):
                c0, n = cols(k)
                c = u * NK + k
                sp.wait_ge(y1_made, (c + 1) * TILES + FREE)
                sp.sem_inc(sp_gate, 1)
                sp.wait_ge(z_made, c * TILES + 1)
                above = (TILES - 1) * GLEN + c0 - TW
                sp.dma_start(SHJ[PITCH:TW, 0:n], G[0:TW - PITCH, above:above + n]).then_inc(shj_in, 16)

            def free_image(u):
                sp.wait_ge(h_inner, u + 1)
                sp.wait_ge(l_inner, u + 1)
                sp.wait_ge(box_step, u * BOX_STEPS + 2)
                sp.sem_inc(sp_gate, 1)
                sp.wait_ge(blk_psum, (u + 1) * PAIRS)

            def unit(u, dst, more, image):
                for k in range(NK):
                    with sp.Fori(0, PAIRS) as i:
                        for par in range(FREE):
                            shift(u, k, 2 * i + par, par)
                    if k == 0 and more:
                        lay_out_features(u + 1)
                    if k >= 1:
                        store_chunk(u, k - 1, dst)
                    shift_strip(u, k)
                store_chunk(u, NK - 1, dst)
                if image is not None:
                    free_image(u + 1)
                    sp.wait_ge(stored, (u + 1) * sum(N_OUT) * 16 + 16)
                    load_image(image)

            def one(tensor, b):
                return tensor[bass.ds(b, 1)].rearrange("o c h w -> (o c) h w")

            sp.sem_inc(stored, 16)
            sp.wait_ge(cleared, CLEARED)
            load_image(x[0])
            lay_out_features(0)
            free_image(0)
            load_image(x[1])
            half = IMAGES // 2
            with sp.Fori(0, half) as b:
                unit(b, one(mid, b), True, one(x, b + half))
            with sp.Fori(0, half) as b:
                unit(b + half, one(mid, b + half), True, one(mid, b))
            with sp.Fori(0, half) as b:
                unit(b + IMAGES, one(out, b), True, one(mid, b + half))
            unit(UNITS - 2, out[IMAGES - 2], True, None)
            unit(UNITS - 1, out[IMAGES - 1], False, None)
            sp.wait_ge(stored, (UNITS * sum(N_OUT) + 1) * 16)

        @block.tensor
        def _(pe):
            pe.sem_inc(z_used, FREE)
            pe.wait_ge(const_in, 32)
            pe.wait_ge(cleared, CLEARED)
            pe.wait_ge(mask_step, 6)
            for t in range(TILES):
                last = pe.matmul(psM[0:TW, 0, 2 * t:2 * t + 2], SQ[0:LAYERS, t * TW:(t + 1) * TW],
                                 idn[0:LAYERS, 0:LAYERS], start=True, stop=True)
            last.then_inc(mask_cols, 1)
            pe.wait_ge(mask_ready, 1)

            def norms(u):
                pe.wait_ge(box_step, (u + 1) * BOX_STEPS)
                pe.wait_ge(lse_rows, u * GROUPS + 1)
                for t in range(TILES):
                    last = pe.matmul(psM[0:TW, 0, t:t + 1], SQ[64:128, t * TW:(t + 1) * TW], ones[64:128, :],
                                     start=True, stop=True)
                last.then_inc(norm_cols, 1)

            def spread(u, col, made, read, start=0):
                for g in range(GROUPS):
                    if g >= 2:
                        pe.wait_ge(read, u * GROUPS + g - 1 + start)
                    for t in range(4 * g, min(4 * g + 4, TILES)):
                        last = pe.matmul(psM[0:TW, g % 2, (t % 4) * TW:(t % 4 + 1) * TW],
                                         col[:, t:t + 1].to_broadcast([TW, TW]), idn[0:TW, 0:TW],
                                         start=True, stop=True)
                    last.then_inc(made, 1)

            def blocks(u):
                for g in range(PAIRS):
                    if g == 0:
                        pe.wait_ge(r_rows, (u + 1) * GROUPS)
                    if g >= 2:
                        pe.wait_ge(blk_l, u * PAIRS + g - 1)
                    for t in (2 * g, 2 * g + 1):
                        for b in range(2):
                            xt = XP[:, t * STRIPS:(t + 1) * STRIPS, :].rearrange("p r w -> p (r w)")[:, b:2 * TW:2]
                            o = (t % 2 * 2 + b) * 128
                            last = pe.transpose(psM[0:TW, g % 2, o:o + 128], xt, idn[:, :])
                    last.then_inc(blk_psum, 1)

            TERMS = [(HL, LH, dy, dx) for dy in range(3) for dx in range(3)]
            TERMS += [(H1, H1, dy, 0) for dy in range(3)]
            TERMS += [(HV, HV, 0, 2), (HL, HL, 2, 2)]

            def score_tile(u, k, t, par):
                s0, w = CHUNKS[k]
                n = w * TW
                pe.wait_ge(g_read, (u * NK + k) * TILES + t + 1)
                for i, (st, mv, dy, dx) in enumerate(TERMS):
                    lo = (s0 + dy) * TW + dx
                    last = pe.matmul(psG[0:TW, par, 0:n], st[:, bass.ds((t + dy) * TW + dx, TW)], mv[:, lo:lo + n],
                                     start=(i == 0), stop=(i == len(TERMS) - 1))
                last.then_inc(g_ready, 1)

            def mirror_tile(u, k, t, par):
                s0, w = CHUNKS[k]
                pe.wait_ge(g_read, (u * NK + k) * TILES + t + 1)
                for i in range(w):
                    at = (s0 + i) * GLEN + (t + 1) * TW
                    last = pe.transpose(psG[0:TW, par, i * TW:(i + 1) * TW], G[:, at:at + TW], idn[0:TW, 0:TW])
                last.then_inc(g_ready, 1)

            def paste_tile(u, k, t, par, order, first=False, end=False):
                n = cols(k)[1]
                z = (u * NK + k) * TILES + order
                pe.wait_ge(zh_made, z + 1 + FREE)
                pe.wait_ge(zl_made, z + 1 + FREE)
                for b in range(2):
                    for i, (w, m) in enumerate(((Bh, Zh), (Bl, Zh), (Bh, Zl))):
                        last = pe.matmul(psO[:, k % 2, b, 0:n],
                                         w[:, bass.ds((2 * t + b) * 128, 128)], m[:, par, 0:n],
                                         start=first and i == 0, stop=end and i == 2)
                last.then_inc(z_used, 1)

            def step(u, z, v, b):
                if z is not None:
                    pe.wait_ge(o_read, (u * NK + z + 1) * 2)

                def pair(i):
                    first, end = isinstance(i, int) and i == 0, isinstance(i, int) and i == PAIRS - 1
                    if b is not None:
                        for par in range(FREE):
                            t = 2 * i + par
                            if isinstance(i, int) and t < CHUNKS[b][0]:
                                mirror_tile(v, b, t, par)
                            else:
                                score_tile(v, b, t, par)
                    if z is not None:
                        paste_tile(u, z, 2 * i + 1, 1, 2 * i, first=first)
                        paste_tile(u, z, 0 if end else 2 * i + 2, 0, 2 * i + 1, end=end)

                lone = max(1, 0 if b is None else -(-CHUNKS[b][0] // 2))
                for i in range(lone):
                    pair(i)
                if lone < PAIRS - 1:
                    with pe.Fori(lone, PAIRS - 1) as i:
                        pair(i)
                pair(PAIRS - 1)

            def scales(v):
                norms(v)
                pe.wait_ge(r_step, (v + 1) * R_STEPS)
                spread(v, R, r_psum, r_rows)

            def log_sums(v):
                pe.wait_ge(lse_dve, (v + 1) * LSE_STEPS)
                pe.wait_ge(blk_l, (v + 1) * PAIRS)
                spread(v, lse, lse_psum, lse_rows, 1)

            def unit(u, more):
                if more:
                    scales(u + 1)
                for k in range(1, NK + 2 if more else NK + 1):
                    if k == 2 and more:
                        pe.wait_ge(f_in, (u + 2) * N_F * 16)
                    if k == NK + 1:
                        blocks(u + 1)
                    step(u, k - 1 if k <= NK else None, u + 1, k - 2 if k >= 2 and more else None)
                if more:
                    log_sums(u + 1)

            scales(0)
            blocks(0)
            pe.wait_ge(f_in, N_F * 16)
            for k in range(NK):
                step(0, None, 0, k)
            log_sums(0)
            with pe.Fori(0, UNITS - 1) as u:
                unit(u, True)
            unit(UNITS - 1, False)

        @block.scalar
        def _(act):
            act.add_instruction(mybir.InstLoadActFuncSet(name=nc.get_next_instruction_name(), engine=act.engine,
                                                         act_func_set_id=EXP_AND_LN))
            act.sem_inc(g_read, FREE)
            act.sem_inc(s_read, FREE)
            act.sem_inc(zh_made, FREE)
            act.sem_inc(o_read, 2 * FREE)
            act.sem_inc(lse_rows, 1)

            def high_features(u):
                act.wait_ge(x_in, (u + 1) * N_X * 16)
                if not (isinstance(u, int) and u == 0):
                    act.wait_ge(f_in, u * N_F * 16)
                    act.wait_ge(g_ready, u * NB)
                act.activation(LH[64:128, TW:TW * (TILES + 1)].rearrange("p (r w) -> p r w", w=PITCH)[:, :, 1:1 + HALF],
                               XP[64:128, :, 1:1 + SIDE:2], ACT.Copy).then_inc(h_inner, 1)
                act.wait_ge(h_inner, u + 1)
                act.activation(LH[64:128, PITCH:TW], LH[64:128, TILES * TW:TILES * TW + 2 * PITCH],
                               ACT.Copy).then_inc(h_made, 1)
                act.activation(LH[64:128, (TILES + 1) * TW:(TILES + 1) * TW + 2 * PITCH], LH[64:128, TW + PITCH:2 * TW],
                               ACT.Copy).then_inc(h_made, 1)

            def read_rows(u, rows, made, read):
                for g in range(GROUPS):
                    act.wait_ge(made, u * GROUPS + g + 1)
                    n = min(4, TILES - 4 * g) * TW
                    act.activation(rows[:, 4 * g * TW:4 * g * TW + n], psM[0:TW, g % 2, 0:n], ACT.Copy).then_inc(read, 1)

            def high_blocks(u):
                act.wait_ge(z_used, u * NB + FREE)
                for g in range(PAIRS):
                    act.wait_ge(blk_psum, u * PAIRS + g + 1)
                    act.activation(Bh[:, g * 512:(g + 1) * 512], psM[0:TW, g % 2, :], ACT.Copy).then_inc(blk_h, 1)

            def score_tile(u, k, t, par):
                c0, n = cols(k, False)
                i = (u * NK + k) * TILES + t
                act.wait_ge(max_made, i + 1)
                if not (isinstance(u, int) and u == 0):
                    act.wait_ge(z_made, (i - NB + TILES + 2) if k < NK - 1 else u * NB + 1)
                act.activation(G[:, bass.ds(t * GLEN + c0, n)], psG[0:TW, par, 0:n], ACT.Copy).then_inc(g_read, 1)
                if k == NK - 1:
                    act.activation(G[:, bass.ds(t * GLEN + c0 + n, WRAP)], G[:, bass.ds(t * GLEN + TW + PITCH, WRAP)], ACT.Copy)
                act.wait_ge(neg_made, i + 1)
                v = S[:, par, :].rearrange("p (s w) -> p s w", w=PITCH)
                parts = [v[:, 0:STRIPS * CHUNKS[k][1], 0:HALF]]
                if k == NK - 1:
                    parts = [v[:, 0:5, 0:HALF], v[:, 6:8, 0:HALF]]
                for j, e in enumerate(parts):
                    last = act.activation(e, e, ACT.Exp, bias=nm[:, bass.ds(k * TILES + t, 1)],
                                          accum_out=sg[:, bass.ds((k + j) * TILES + t, 1)])
                last.then_inc(s_read, 1)

            def softmax_tile(u, k, t):
                c0, n = cols(k)
                i = (u * NK + k) * TILES + t
                act.wait_ge(arg_made, i + 2)
                y = G[:, bass.ds(t * GLEN + c0, n)]
                act.activation(y, y, ACT.Exp, bias=nb[:, bass.ds(u * TILES + t, 1)]).then_inc(y_made, 1)

            def high_z(u, k, par, order):
                z = (u * NK + k) * TILES + order
                n = cols(k)[1]
                act.wait_ge(z_made, z + 2)
                act.wait_ge(z_used, z + 1)
                act.activation(Zh[:, par, 0:n], Z[:, par, 0:n], ACT.Copy, scale=ZSCALE).then_inc(zh_made, 1)

            def read_out(u, k):
                c = u * NK + k
                n = cols(k)[1]
                act.wait_ge(z_used, (c + 1) * TILES + FREE)
                act.wait_ge(stored, (u * sum(N_OUT) + sum(N_OUT[:k]) + 1) * 16)
                for b in range(2):
                    act.activation(OSB[:, 0:n // PITCH, b:b + 2 * HALF + 1:2],
                                   psO[:, k % 2, b, 0:n].rearrange("p (s w) -> p s w", w=PITCH)[:, :, 0:HALF + 1],
                                   ACT.Copy, scale=0.25 / ZSCALE).then_inc(o_read, 1)

            def step(u, f, z, v, b):
                with act.Fori(0, PAIRS) as i:
                    if z is not None:
                        high_z(u, z, 1, 2 * i)
                        high_z(u, z, 0, 2 * i + 1)
                    if f is not None:
                        softmax_tile(u, f, 2 * i)
                        softmax_tile(u, f, 2 * i + 1)
                    if b is not None:
                        for par in range(FREE):
                            score_tile(v, b, 2 * i + par, par)
                if z is not None:
                    read_out(u, z)

            def scales(v):
                act.wait_ge(r_step, v * R_STEPS + 1)
                act.activation(lnn[:, :], nsq[:, :], ACT.Ln).then_inc(root_made, 1)
                act.wait_ge(root_made, 2 * v + 1)
                act.activation(root[:, :], lnn[:, :], ACT.Exp, scale=0.5).then_inc(root_made, 1)
                read_rows(v, RB, r_psum, r_rows)

            def log_sums(v):
                act.wait_ge(lse_dve, v * LSE_STEPS + 2)
                act.activation(ed[:, :], df[:, :], ACT.Exp).then_inc(lse_act, 1)
                act.wait_ge(lse_dve, v * LSE_STEPS + 4)
                act.activation(lns[:, :], tot[:, :], ACT.Ln).then_inc(lse_act, 1)
                read_rows(v, BC, lse_psum, lse_rows)
                act.wait_ge(lse_rows, (v + 1) * GROUPS + 1)
                act.activation(BC[:, TILES * TW:CLEN], BC[:, PITCH:TW], ACT.Copy).then_inc(lse_wrap, 1)

            def unit(u, more):
                step(u, 0, None, None, None)
                if more:
                    high_features(u + 1)
                    scales(u + 1)
                for k in range(1, NK + 2 if more else NK + 1):
                    if k == NK + 1:
                        high_blocks(u + 1)
                    step(u, k if k < NK else None, k - 1 if k <= NK else None, u + 1, k - 2 if k >= 2 and more else None)
                if more:
                    log_sums(u + 1)

            act.wait_ge(cleared, CLEARED)
            high_features(0)
            scales(0)
            high_blocks(0)
            for k in range(NK):
                step(0, None, None, 0, k)
            log_sums(0)
            with act.Fori(0, UNITS - 1) as u:
                unit(u, True)
            unit(UNITS - 1, False)

        def box_sums(eng, p0, p1, step, base):
            wide, tall = (TILES + 2) * TW, TILES * TW
            sq, bx = SQ[p0:p1, :], BX[p0:p1, :]
            eng.tensor_tensor(bx[:, 0:wide], sq[:, 0:wide], sq[:, 1:wide + 1], ALU.add).then_inc(step, 1)
            eng.wait_ge(step, base + 1)
            eng.tensor_tensor(bx[:, 0:wide], bx[:, 0:wide], sq[:, 2:wide + 2], ALU.add).then_inc(step, 1)
            eng.wait_ge(step, base + 2)
            eng.tensor_tensor(sq[:, 0:tall], bx[:, 0:tall], bx[:, TW:TW + tall], ALU.add).then_inc(step, 1)
            eng.wait_ge(step, base + 3)
            eng.tensor_tensor(sq[:, 0:tall], sq[:, 0:tall], bx[:, 2 * TW:2 * TW + tall], ALU.add).then_inc(step, 1)

        @block.vector
        def _(dve):
            for tile, value in ((XP[:, :, :], 0.0), (HL[:, :].bitcast(F32), 0.0), (LH[:, :].bitcast(F32), 0.0),
                                (H1[:, :].bitcast(F32), 0.0), (HV[:, :].bitcast(F32), 0.0), (ones[:, :], 1.0),
                                (SH[:, :, :], 0.0), (SHJ[:, :], 0.0)):
                dve.memset(tile, value).then_inc(cleared, 1)
            dve.sem_inc(zl_made, FREE)
            dve.sem_inc(arg_made, 1)
            dve.sem_inc(z_made, 1)
            dve.memset(SQ[0:LAYERS, :], 0.0).then_inc(mask_step, 1)
            dve.wait_ge(mask_in, 32)
            dve.wait_ge(mask_step, 1)
            m = G[0:LAYERS, 0:SIDE * SIDE].rearrange("p (h w) -> p h w", w=SIDE)
            f = SQ[0:LAYERS, 0:FROWS * TW].rearrange("p (r j w) -> p j r w", j=STRIPS, w=PITCH)
            for j in range(STRIPS):
                lo, hi = max(TILES * j - 1, 0), min(TILES * j + TILES + 1, HALF)
                r = lo - (TILES * j - 1)
                last = dve.tensor_copy(f[:, j, r:r + hi - lo, 1:1 + HALF], m[:, 2 * lo:2 * hi:2, 0:SIDE:2])
            last.then_inc(mask_step, 1)
            dve.wait_ge(mask_step, 2)
            box_sums(dve, 0, LAYERS, mask_step, 2)
            dve.memset(G[:, :].rearrange("p (t c) -> p t c", c=GLEN)[:, :, 0:TW], 0.0)
            dve.wait_ge(mask_cols, 1)
            dve.wait_ge(const_in, 32)
            dve.tensor_scalar(mmc[:, :, :], psM[0:TW, 0, 0:LAYERS * TILES].rearrange("p (t l) -> p l t", l=LAYERS),
                              0.0, None, ALU.is_equal).then_inc(mask_ready, 1)
            dve.wait_ge(mask_ready, 1)
            for layer in range(LAYERS):
                last = dve.tensor_tensor(mmc[:, layer, :], mmc[:, layer, :], vld[:, :], ALU.mult)
            last.then_inc(mask_ready, 1)
            dve.wait_ge(mask_ready, 2)
            for u in range(UNITS):
                at = slice(u * TILES, (u + 1) * TILES)
                dve.tensor_scalar(mm20[:, at], mmc[:, u // IMAGES, :], 20.0, None, ALU.mult).then_inc(mask_ready, 1)
                dve.tensor_scalar(nb[:, at], mmc[:, u // IMAGES, :], -1.0, BIG, ALU.add, ALU.mult).then_inc(mask_ready, 1)
            dve.tensor_scalar(big[:, :], vld[:, :], -2.0 * BIG, BIG, ALU.mult, ALU.add).then_inc(mask_ready, 1)
            dve.wait_ge(mask_ready, 2 + 2 * UNITS + 1)

            def low_features(u):
                dve.wait_ge(h_inner, u + 1)
                inner = lambda a: a[64:128, TW:TW * (TILES + 1)].rearrange("p (r w) -> p r w", w=PITCH)[:, :, 1:1 + HALF]
                dve.tensor_tensor(inner(HL), XP[64:128, :, 1:1 + SIDE:2], inner(LH), ALU.subtract).then_inc(l_inner, 1)
                dve.wait_ge(l_inner, u + 1)
                dve.tensor_copy(HL[64:128, PITCH:TW], HL[64:128, TILES * TW:TILES * TW + 2 * PITCH]).then_inc(l_made, 1)
                dve.tensor_copy(HL[64:128, (TILES + 1) * TW:(TILES + 1) * TW + 2 * PITCH],
                                HL[64:128, TW + PITCH:2 * TW]).then_inc(l_made, 1)

            def scales(u):
                dve.wait_ge(norm_cols, u + 1)
                at = u * R_STEPS
                dve.tensor_scalar(nsq[:, :], psM[0:TW, 0, 0:TILES], 1e-8, None, ALU.max).then_inc(r_step, 1)
                dve.wait_ge(root_made, 2 * (u + 1))
                dve.reciprocal(rcp[:, :], root[:, :]).then_inc(r_step, 1)
                dve.wait_ge(r_step, at + 2)
                dve.tensor_tensor(quo[:, :], nsq[:, :], rcp[:, :], ALU.mult).then_inc(r_step, 1)
                dve.wait_ge(r_step, at + 3)
                dve.tensor_tensor(nrm2[:, :], quo[:, :], root[:, :], ALU.add).then_inc(r_step, 1)
                dve.wait_ge(r_step, at + 4)
                dve.reciprocal(rcp[:, :], nrm2[:, :]).then_inc(r_step, 1)
                dve.wait_ge(r_step, at + 5)
                mm = mm20[:, bass.ds(u * TILES, TILES)]
                dve.tensor_tensor(R[:, :], rcp[:, :], mm, ALU.mult).then_inc(r_step, 1)
                dve.tensor_tensor(RA[:, bass.ds(u * TILES, TILES)], rcp[:, :], mm, ALU.mult).then_inc(r_step, 1)

            def low_blocks(u):
                for g in range(PAIRS):
                    dve.wait_ge(blk_h, u * PAIRS + g + 1)
                    at = slice(g * 512, (g + 1) * 512)
                    dve.tensor_tensor(Bl[:, at], psM[0:TW, g % 2, :], Bh[:, at], ALU.subtract).then_inc(blk_l, 1)

            def score_tile(u, k, t, par):
                s0, w = CHUNKS[k]
                n = w * TW
                i = (u * NK + k) * TILES + t
                dve.wait_ge(g_ready, i + 1)
                dve.wait_ge(s_read, i + 1)
                dve.sem_inc(dve_gate, 1)
                dve.tensor_tensor_reduce(S[:, par, 0:n], psG[0:TW, par, 0:n], RB[:, s0 * TW:s0 * TW + n], 1.0, 0.0,
                                         ALU.mult, ALU.max, mx[:, par:par + 1]).then_inc(max_made, 1)
                dve.wait_ge(max_made, i + 1)
                dve.tensor_scalar(nm[:, bass.ds(k * TILES + t, 1)], mx[:, par:par + 1], -1.0, None,
                                  ALU.mult).then_inc(neg_made, 1)

            def log_sums(u):
                at = u * LSE_STEPS
                by_tile = lambda a: a.rearrange("p (k t) -> p t k", t=TILES)
                dve.wait_ge(s_read, (u + 1) * NB + FREE)
                last = slice((NK - 1) * TILES, NK * TILES)
                dve.tensor_reduce(nM[:, :], by_tile(nm[:, :]), AX.X, ALU.min).then_inc(lse_dve, 1)
                dve.tensor_tensor(sg[:, last], sg[:, last], sg[:, NK * TILES:], ALU.add)
                dve.wait_ge(lse_dve, at + 1)
                dve.tensor_tensor(df[:, :].rearrange("p (k t) -> p k t", t=TILES),
                                  nM[:, :].unsqueeze(1).to_broadcast([TW, NK, TILES]),
                                  nm[:, :].rearrange("p (k t) -> p k t", t=TILES), ALU.subtract).then_inc(lse_dve, 1)
                dve.wait_ge(lse_act, u * 2 + 1)
                dve.tensor_tensor(df[:, :], ed[:, :], sg[:, 0:NK * TILES], ALU.mult).then_inc(lse_dve, 1)
                dve.wait_ge(lse_dve, at + 3)
                dve.tensor_reduce(tot[:, :], by_tile(df[:, :]), AX.X, ALU.add).then_inc(lse_dve, 1)
                dve.wait_ge(lse_act, u * 2 + 2)
                dve.tensor_tensor(tot[:, :], lns[:, :], nM[:, :], ALU.subtract).then_inc(lse_dve, 1)
                dve.wait_ge(lse_dve, at + 5)
                dve.tensor_tensor(lse[:, :], tot[:, :], big[:, :], ALU.max).then_inc(lse_dve, 1)

            def argument(u, k, t):
                c0, n = cols(k)
                g = G[:, bass.ds(t * GLEN + c0, n)]
                dve.scalar_tensor_tensor(out=g, in0=g, scalar=RA[:, bass.ds(u * TILES + t, 1)], in1=BC[:, c0 - TW:c0 - TW + n],
                                         op0=ALU.mult, op1=ALU.subtract).then_inc(arg_made, 1)

            def sum_z(u, k, t, par, order):
                c0, n = cols(k)
                c = u * NK + k
                if isinstance(t, int) and t == 0:
                    dve.wait_ge(shj_in, (c + 1) * 16)
                    above = SHJ[:, 0:n]
                else:
                    dve.wait_ge(y1_made, c * TILES + t + 1 + FREE)
                    above = G[:, bass.ds((t - 1) * GLEN + c0 - TW, n)]
                dve.wait_ge(zh_made, c * TILES + order + 1)
                dve.wait_ge(zl_made, c * TILES + order + 1)
                dve.tensor_tensor(Z[:, par, 0:n], G[:, bass.ds(t * GLEN + c0, n)], above, ALU.add).then_inc(z_made, 1)

            def low_z(u, k, par, order):
                n = cols(k)[1]
                dve.wait_ge(zh_made, (u * NK + k) * TILES + order + 1 + FREE)
                dve.scalar_tensor_tensor(out=Zl[:, par, 0:n], in0=Z[:, par, 0:n], scalar=ZSCALE, in1=Zh[:, par, 0:n],
                                         op0=ALU.mult, op1=ALU.subtract).then_inc(zl_made, 1)

            def step(u, f, z, v, b):
                def pair(i):
                    end = isinstance(i, int)
                    if z is not None:
                        sum_z(u, z, 2 * i + 1, 1, 2 * i)
                        sum_z(u, z, 0 if end else 2 * i + 2, 0, 2 * i + 1)
                    if f is not None:
                        argument(u, f, 2 * i)
                        argument(u, f, 2 * i + 1)
                    if z is not None:
                        low_z(u, z, 1, 2 * i)
                        low_z(u, z, 0, 2 * i + 1)
                    if b is not None:
                        for par in range(FREE):
                            score_tile(v, b, 2 * i + par, par)

                with dve.Fori(0, PAIRS - 1) as i:
                    pair(i)
                pair(PAIRS - 1)

            def unit(u, more):
                dve.wait_ge(lse_wrap, u + 1)
                dve.sem_inc(dve_gate, 1)
                step(u, 0, None, None, None)
                if more:
                    low_features(u + 1)
                    scales(u + 1)
                for k in range(1, NK + 2 if more else NK + 1):
                    if k == 2 and more:
                        dve.wait_ge(r_rows, (u + 2) * GROUPS)
                        dve.sem_inc(dve_gate, 1)
                    if k == NK + 1:
                        low_blocks(u + 1)
                    step(u, k if k < NK else None, k - 1 if k <= NK else None, u + 1, k - 2 if k >= 2 and more else None)
                if more:
                    log_sums(u + 1)

            low_features(0)
            scales(0)
            low_blocks(0)
            dve.wait_ge(r_rows, GROUPS)
            dve.sem_inc(dve_gate, 1)
            for k in range(NK):
                step(0, None, None, 0, k)
            log_sums(0)
            with dve.Fori(0, UNITS - 1) as u:
                unit(u, True)
            unit(UNITS - 1, False)

        @block.gpsimd
        def _(pool):
            for tile in (SQ[64:128, :], BX[64:128, :]):
                pool.memset(tile, 0.0).then_inc(cleared, 1)
            pool.sem_inc(y1_made, FREE)

            def squares(u):
                at = u * BOX_STEPS
                if not (isinstance(u, int) and u == 0):
                    pool.wait_ge(norm_cols, u)
                pool.wait_ge(x_in, (u + 1) * N_X * 16)
                pool.sem_inc(pool_gate, 1)
                pool.memset(SQ[64:128, :], 0.0).then_inc(box_step, 1)
                pool.wait_ge(box_step, at + 1)
                f = XP[64:128, :, 1:1 + SIDE:2]
                pool.tensor_tensor(SQ[64:128, TW:TW * (TILES + 1)].rearrange("p (r w) -> p r w", w=PITCH)[:, :, 1:1 + HALF],
                                   f, f, ALU.mult).then_inc(box_step, 1)
                pool.wait_ge(box_step, at + 2)
                pool.sem_inc(pool_gate, 1)
                pool.tensor_copy(SQ[64:128, PITCH:TW], SQ[64:128, TILES * TW:TILES * TW + 2 * PITCH]).then_inc(box_step, 1)
                pool.tensor_copy(SQ[64:128, (TILES + 1) * TW:(TILES + 1) * TW + 2 * PITCH],
                                 SQ[64:128, TW + PITCH:2 * TW]).then_inc(box_step, 1)
                pool.wait_ge(box_step, at + 4)
                box_sums(pool, 64, 128, box_step, at + 4)

            def sum_y1(u, k, t, par, i):
                c0, n = cols(k)
                pool.wait_ge(sh_in[par], ((u * NK + k) * PAIRS + i + 1) * 16)
                g = G[:, bass.ds(t * GLEN + c0, n)]
                pool.tensor_tensor(g, g, SH[:, par, 0:n], ALU.add).then_inc(y1_made, 1)

            def unit(u, image):
                for k in range(NK):
                    with pool.Fori(0, PAIRS) as i:
                        for par in range(FREE):
                            sum_y1(u, k, 2 * i + par, par, i)
                if image:
                    pool.wait_ge(y1_made, (u + 1) * NB + FREE)
                    squares(u + 2)
                    pool.wait_ge(box_step, (u + 3) * BOX_STEPS)
                    pool.sem_inc(pool_gate, 1)

            pool.wait_ge(cleared, CLEARED)
            squares(0)
            squares(1)
            pool.wait_ge(box_step, 2 * BOX_STEPS)
            with pool.Fori(0, UNITS - 2) as u:
                unit(u, True)
            unit(UNITS - 2, False)
            unit(UNITS - 1, False)


def kernel(x, L0_conv_mask, L1_conv_mask):
    import numpy as np
    import concourse.bacc as bacc
    from concourse.bass_utils import run_bass_kernel_spmd

    nc = bacc.Bacc("TRN2", target_bir_lowering=False, num_devices=1)
    rows = np.arange(TW) // PITCH * TILES
    valid = (rows[:, None] + np.arange(TILES)[None, :] < HALF) & (np.arange(TW) % PITCH < HALF)[:, None]
    arrays = {
        "x": np.ascontiguousarray(x),
        "mask0": np.ascontiguousarray(L0_conv_mask),
        "mask1": np.ascontiguousarray(L1_conv_mask),
        "ident": np.eye(128, dtype=np.float32),
        "valid": valid.astype(np.float32),
    }
    ins = [nc.dram_tensor(n, a.shape, mybir.dt.from_np(a.dtype), kind="ExternalInput").ap() for n, a in arrays.items()]
    out = nc.dram_tensor("out", (IMAGES, C, SIDE, SIDE), F32, kind="ExternalOutput").ap()
    contextual_attention(nc, *ins, out)
    return run_bass_kernel_spmd(nc, [arrays], core_ids=[0]).results[0]["out"]
```

```python
from contextlib import ExitStack

import concourse.bass as bass
from concourse import mybir

F32 = mybir.dt.float32
F16 = mybir.dt.float16
ALU = mybir.AluOpType
ACT = mybir.ActivationFunctionType
AX = mybir.AxisListType

LAYERS, IMAGES, C, SIDE = 2, 4, 64, 80
UNITS = LAYERS * IMAGES
HALF = SIDE // 2
STRIPS, TILES = 3, 14
PITCH = HALF + 2
TW = STRIPS * PITCH
FROWS = TILES + 2
FLEN = FROWS * TW + 4
HT = TILES // 2
WRAP = 2 * PITCH
CLEN = TILES * TW + WRAP
GLEN = TW + CLEN
CHUNKS = [(0, 4), (4, 4), (8, 3), (11, 3)]
NK = len(CHUNKS)
ZSCALE = 4096.0
BIG = 1.0e30
FREE = 2
ZFREE = 4
SFREE = 4
EXP_AND_LN = 6


def contextual_attention(nc, x, mask0, mask1, ident, valid, out):
    mid = nc.dram_tensor("mid", (IMAGES, C, SIDE, SIDE), F32, kind="Internal").ap()

    with ExitStack() as ctx:
        def sb(name, shape, dt):
            return ctx.enter_context(nc.sbuf_tensor(name, shape, dt))

        def ps(name, shape):
            return ctx.enter_context(nc.psum_tensor(name, shape, F32))

        def sem(name):
            return ctx.enter_context(nc.semaphore(name))

        G = sb("G", [TW, TILES * GLEN], F32)
        HL = sb("HL", [128, FLEN], F16)
        LH = sb("LH", [128, FLEN], F16)
        H1 = sb("H1", [128, FLEN], F16)
        HV = sb("HV", [128, FLEN], F16)
        XP = sb("XP", [128, TILES * STRIPS, 2 * PITCH], F32)
        Bh = sb("Bh", [TW, TILES * 2 * 128], F16)
        Bl = sb("Bl", [TW, TILES * 2 * 128], F16)
        SQ = sb("SQ", [128, FLEN], F32)
        RB = sb("RB", [TW, TILES * TW], F32)
        BC = sb("BC", [TW, CLEN], F32)
        SH = sb("SH", [TW, SFREE, 4 * TW], F32)
        SHJ = sb("SHJ", [TW, 4 * TW], F32)
        Z = sb("Z", [TW, FREE, 4 * TW], F32)
        Zh = sb("Zh", [TW, ZFREE, 4 * TW], F16)
        Zl = sb("Zl", [TW, ZFREE, 4 * TW], F16)
        BX = sb("BX", [128, FROWS * TW], F32)
        S = BX[0:TW, 0:FREE * 4 * TW].rearrange("p (r n) -> p r n", r=FREE)
        OSB = BX[:, FREE * 4 * TW:].rearrange("p (s w) -> p s w", w=2 * PITCH)
        idn = sb("idn", [128, 128], F32)
        ones = sb("ones", [128, 1], F32)
        vld = sb("vld", [TW, TILES], F32)
        big = sb("big", [TW, TILES], F32)
        mm20 = sb("mm20", [TW, UNITS * TILES], F32)
        nb = sb("nb", [TW, UNITS * TILES], F32)
        mmc = sb("mmc", [TW, LAYERS, TILES], F32)
        nsq = sb("nsq", [TW, TILES], F32)
        root = sb("root", [TW, TILES], F32)
        lnn = sb("lnn", [TW, TILES], F32)
        quo = sb("quo", [TW, TILES], F32)
        nrm2 = sb("nrm2", [TW, TILES], F32)
        rcp = sb("rcp", [TW, TILES], F32)
        R = sb("R", [TW, TILES], F32)
        RA = sb("RA", [TW, UNITS * TILES], F32)
        mx = sb("mx", [TW, FREE], F32)
        nm = sb("nm", [TW, NK * TILES], F32)
        sg = sb("sg", [TW, (NK + 1) * TILES], F32)
        nM = sb("nM", [TW, TILES], F32)
        df = sb("df", [TW, NK * TILES], F32)
        ed = sb("ed", [TW, NK * TILES], F32)
        tot = sb("tot", [TW, TILES], F32)
        lns = sb("lns", [TW, TILES], F32)
        lse = sb("lse", [TW, TILES], F32)

        psG = ps("psG", [128, FREE, 512])
        psO = ps("psO", [128, FREE, 2, 512])
        psM = ps("psM", [128, FREE, 512])

        const_in = sem("const_in")
        cleared = sem("cleared")
        mask_in = sem("mask_in")
        mask_step = sem("mask_step")
        mask_cols = sem("mask_cols")
        mask_ready = sem("mask_ready")
        x_in = sem("x_in")
        h_inner = sem("h_inner")
        h_made = sem("h_made")
        l_inner = sem("l_inner")
        l_made = sem("l_made")
        f_in = sem("f_in")
        sq_made = sem("sq_made")
        box_step = sem("box_step")
        norm_cols = sem("norm_cols")
        r_step = sem("r_step")
        root_made = sem("root_made")
        r_psum = sem("r_psum")
        r_rows = sem("r_rows")
        blk_psum = sem("blk_psum")
        blk_h = sem("blk_h")
        blk_l = sem("blk_l")
        g_ready = sem("g_ready")
        g_read = sem("g_read")
        max_made = sem("max_made")
        act_gate = sem("act_gate")
        dve_gate = sem("dve_gate")
        pe_gate = sem("pe_gate")
        sp_gate = sem("sp_gate")
        pool_gate = sem("pool_gate")
        neg_made = sem("neg_made")
        s_read = sem("s_read")
        lse_dve = sem("lse_dve")
        lse_act = sem("lse_act")
        lse_psum = sem("lse_psum")
        lse_rows = sem("lse_rows")
        lse_wrap = sem("lse_wrap")
        wrap_made = sem("wrap_made")
        arg_made = sem("arg_made")
        y_made = sem("y_made")
        sh_in = [sem(f"sh_in{i}") for i in range(SFREE)]
        shj_in = sem("shj_in")
        y1_made = sem("y1_made")
        z_made = sem("z_made")
        zh_made = sem("zh_made")
        zl_made = sem("zl_made")
        z_used = sem("z_used")
        o_read = sem("o_read")
        stored = sem("stored")

        NB = NK * TILES
        GROUPS = 4
        PAIRS = TILES // 2
        CLEARED = 11
        SQ_STEPS = 4
        BOX_STEPS = 4
        R_STEPS = 7
        LSE_STEPS = 6

        def cols(k, wrap=True):
            s0, n = CHUNKS[k]
            return (s0 + 1) * TW, n * TW + (WRAP if wrap and k == NK - 1 else 0)

        def out_parts(k):
            s0, n = CHUNKS[k]
            for j in range(STRIPS):
                q = [TILES * j + s for s in range(s0, s0 + n + (k == NK - 1)) if s > 0 or j == 0]
                for a in range(2):
                    rows = [r for r in q if 1 - a <= r <= HALF - a]
                    if rows:
                        yield a, j, rows[0] - TILES * j - s0, len(rows), rows[0] - 1 + a

        def pair_of(k, i):
            return (i + PAIRS - 2) % PAIRS if k == NK - 1 else i

        def block_groups(i):
            return [g for g in (2 * i, 2 * i + 1) if g < PAIRS]

        N_OUT = [len(list(out_parts(k))) for k in range(NK)]
        N_X = 6
        N_F = 6

        block = ctx.enter_context(nc.Block())

        @block.sync
        def _(sp):
            sp.dma_start(idn[:, :], ident).then_inc(const_in, 16)
            sp.dma_start(vld[:, :], valid).then_inc(const_in, 16)
            for layer, m in enumerate((mask0, mask1)):
                sp.dma_start(G[layer:layer + 1, 0:SIDE * SIDE],
                             m.rearrange("o c h w -> (o c) (h w)")).then_inc(mask_in, 16)

            def load_image(src):
                for a in range(2):
                    rows = src.rearrange("c (h two) w -> two c h w", two=2)[1 - a]
                    v = XP[64 * a:64 * a + 64, :, :].rearrange("p (t j) w -> p j t w", j=STRIPS)
                    for j in range(STRIPS):
                        lo, hi = max(TILES * j, 1 - a), min(TILES * (j + 1), HALF + 1 - a)
                        h = lo - 1 + a
                        sp.dma_start(v[:, j, lo - TILES * j:hi - TILES * j, 1:1 + SIDE],
                                     rows[:, h:h + hi - lo, :]).then_inc(x_in, 16)

            def lay_out_features(u):
                sp.wait_ge(h_made, 2 * (u + 1))
                sp.wait_ge(l_made, 2 * (u + 1))
                up, n = slice(64, 128), FLEN
                for dst, src in ((HL[0:64, :], LH[up, :]), (LH[0:64, :], HL[up, :]),
                                 (H1[0:64, :], LH[up, :]), (H1[up, 0:n - 1], LH[up, 1:n]),
                                 (HV[0:64, :], LH[up, :]), (HV[up, 0:n - TW], LH[up, TW:n])):
                    sp.dma_start(dst, src).then_inc(f_in, 16)

            def store_chunk(u, k, dst):
                sp.wait_ge(o_read, (u * NK + k + 1) * 2 + 2 * FREE)
                v = OSB[:, :, :].rearrange("p (s j) w -> p j s w", j=STRIPS)
                for a, j, s, n, h in out_parts(k):
                    rows = dst.rearrange("c (h two) w -> two c h w", two=2)[1 - a]
                    sp.dma_start(rows[:, h:h + n, :],
                                 v[64 * a:64 * a + 64, j, s:s + n, 1:1 + SIDE]).then_inc(stored, 16)

            def shift(u, k, t, slot):
                c0, n = cols(k)
                i = (u * NK + k) * TILES + t
                sp.wait_ge(y_made, i + 1)
                sp.wait_ge(y1_made, i + 1)
                sp.dma_start(SH[1:TW, slot, 1:n], G[0:TW - 1, bass.ds(t * GLEN + c0, n - 1)]).then_inc(sh_in[slot], 16)

            def shift_strip(u, k):
                c0, n = cols(k)
                c = u * NK + k
                sp.wait_ge(y1_made, (c + 1) * TILES + SFREE)
                sp.sem_inc(sp_gate, 1)
                sp.wait_ge(z_made, c * TILES + 1)
                above = (TILES - 1) * GLEN + c0 - TW
                sp.dma_start(SHJ[PITCH:TW, 0:n], G[0:TW - PITCH, above:above + n]).then_inc(shj_in, 16)

            def free_image(u):
                sp.wait_ge(h_inner, u + 1)
                sp.wait_ge(l_inner, u + 1)
                sp.sem_inc(sp_gate, 1)
                sp.wait_ge(sq_made, (u + 1) * SQ_STEPS)
                sp.sem_inc(sp_gate, 1)
                sp.wait_ge(blk_psum, (u + 1) * PAIRS)

            def unit(u, dst, more, image):
                for k in range(NK):
                    with sp.Fori(0, PAIRS // 2) as i:
                        for t in range(4):
                            shift(u, k, 4 * i + t, (2 * k + t) % SFREE)
                    for t in (TILES - 2, TILES - 1):
                        shift(u, k, t, (2 * k + t) % SFREE)
                    if k == 0 and more:
                        lay_out_features(u + 1)
                    if k >= 1:
                        store_chunk(u, k - 1, dst)
                    shift_strip(u, k)
                store_chunk(u, NK - 1, dst)
                if image is not None:
                    free_image(u + 1)
                    sp.wait_ge(stored, (u + 1) * sum(N_OUT) * 16 + 16)
                    load_image(image)

            def one(tensor, b):
                return tensor[bass.ds(b, 1)].rearrange("o c h w -> (o c) h w")

            sp.sem_inc(stored, 16)
            sp.wait_ge(cleared, CLEARED)
            load_image(x[0])
            lay_out_features(0)
            free_image(0)
            load_image(x[1])
            half = IMAGES // 2
            with sp.Fori(0, half) as b:
                unit(b, one(mid, b), True, one(x, b + half))
            with sp.Fori(0, half) as b:
                unit(b + half, one(mid, b + half), True, one(mid, b))
            with sp.Fori(0, half) as b:
                unit(b + IMAGES, one(out, b), True, one(mid, b + half))
            unit(UNITS - 2, out[IMAGES - 2], True, None)
            unit(UNITS - 1, out[IMAGES - 1], False, None)
            sp.wait_ge(stored, (UNITS * sum(N_OUT) + 1) * 16)

        @block.tensor
        def _(pe):
            pe.sem_inc(z_used, ZFREE)
            pe.wait_ge(const_in, 32)
            pe.wait_ge(cleared, CLEARED)
            pe.wait_ge(mask_step, 6)
            for t in range(TILES):
                last = pe.matmul(psM[0:TW, 0, 2 * t:2 * t + 2], SQ[0:LAYERS, t * TW:(t + 1) * TW],
                                 idn[0:LAYERS, 0:LAYERS], start=True, stop=True)
            last.then_inc(mask_cols, 1)
            pe.wait_ge(mask_ready, 2)

            def norms(u):
                pe.wait_ge(box_step, (u + 1) * BOX_STEPS)
                pe.wait_ge(lse_rows, u * GROUPS + 1)
                for t in range(TILES):
                    p0, row = (0, t) if t < HT else (64, t - HT)
                    at = (HT + 2 + row) * TW
                    last = pe.matmul(psM[0:TW, t // HT, row:row + 1], BX[p0:p0 + 64, at:at + TW], ones[p0:p0 + 64, :],
                                     start=True, stop=True)
                last.then_inc(norm_cols, 1)

            def spread(u, col, made, read, start=0):
                for g in range(GROUPS):
                    if g >= 2:
                        pe.wait_ge(read, u * GROUPS + g - 1 + start)
                    for t in range(4 * g, min(4 * g + 4, TILES)):
                        last = pe.matmul(psM[0:TW, g % 2, (t % 4) * TW:(t % 4 + 1) * TW],
                                         col[:, t:t + 1].to_broadcast([TW, TW]), idn[0:TW, 0:TW],
                                         start=True, stop=True)
                    last.then_inc(made, 1)

            def block_group(u, g):
                if g == 0:
                    pe.wait_ge(r_rows, (u + 1) * GROUPS)
                if g >= 2:
                    pe.wait_ge(blk_l, u * PAIRS + g - 1)
                for t in (2 * g, 2 * g + 1):
                    for b in range(2):
                        xt = XP[:, t * STRIPS:(t + 1) * STRIPS, :].rearrange("p r w -> p (r w)")[:, b:2 * TW:2]
                        o = (t % 2 * 2 + b) * 128
                        last = pe.transpose(psM[0:TW, g % 2, o:o + 128], xt, idn[:, :])
                last.then_inc(blk_psum, 1)

            TERMS = [(HL, LH, dy, dx) for dy in range(3) for dx in range(3)]
            TERMS += [(H1, H1, dy, 0) for dy in range(3)]
            TERMS += [(HV, HV, 0, 2), (HL, HL, 2, 2)]

            def score_tile(u, k, t, par, at):
                s0, w = CHUNKS[k]
                stored = 0
                if isinstance(t, int):
                    first = s0 if s0 % 2 == 0 else s0 - 1
                    stored = w if t < s0 else max(0, t // 2 * 2 - s0) if t < s0 + w else 0
                    if stored and (t == first + 2 or (k == NK - 1 and at == 0)):
                        pe.wait_ge(g_read, (u * NK + k) * TILES + at + FREE)
                pe.wait_ge(g_read, (u * NK + k) * TILES + at + 1)
                for i in range(stored):
                    c = (s0 + i) * GLEN + (t + 1) * TW
                    last = pe.transpose(psG[0:TW, par, i * TW:(i + 1) * TW], G[:, c:c + TW], idn[0:TW, 0:TW])
                n = (w - stored) * TW
                for i, (st, mv, dy, dx) in enumerate(TERMS if n else ()):
                    lo = (s0 + stored + dy) * TW + dx
                    last = pe.matmul(psG[0:TW, par, stored * TW:w * TW], st[:, bass.ds((t + dy) * TW + dx, TW)],
                                     mv[:, lo:lo + n], start=(i == 0), stop=(i == len(TERMS) - 1))
                last.then_inc(g_ready, 1)

            def paste_tile(u, k, t, par, order, first=False, end=False):
                n = cols(k)[1]
                z = (u * NK + k) * TILES + order
                pe.wait_ge(zl_made, z + 1 + FREE)
                for b in range(2):
                    for i, (w, m) in enumerate(((Bh, Zh), (Bl, Zh), (Bh, Zl))):
                        last = pe.matmul(psO[:, k % 2, b, 0:n],
                                         w[:, bass.ds((2 * t + b) * 128, 128)], m[:, par, 0:n],
                                         start=first and i == 0, stop=end and i == 2)
                last.then_inc(z_used, 1)

            def step(u, z, v, b, more=True):
                if z is not None:
                    pe.wait_ge(o_read, (u * NK + z + 1) * 2)

                def pair(i, odd):
                    first, end = isinstance(i, int) and i == 0, isinstance(i, int) and i == PAIRS - 1
                    if b is not None:
                        for par in range(FREE):
                            score_tile(v, b, 2 * pair_of(b, i) + par, par, 2 * i + par)
                    if z is not None:
                        slot = 2 * ((z + odd) % 2)
                        paste_tile(u, z, 2 * i + 1, slot, 2 * i, first=first)
                        paste_tile(u, z, 0 if end else 2 * i + 2, slot + 1, 2 * i + 1, end=end)
                    if z is None and b == NK - 1:
                        for g in block_groups(i):
                            block_group(v, g)

                lone = 2 if b is None else min(PAIRS - 1, (sum(CHUNKS[b]) + 3) // 4 * 2)
                if z == 0 and more:
                    lone = 4
                for i in range(lone):
                    pair(i, i % 2)
                if z == 0 and more:
                    norms(v)
                if lone < PAIRS - 1:
                    with pe.Fori(lone // 2, PAIRS // 2) as i:
                        pair(2 * i, 0)
                        pair(2 * i + 1, 1)
                if z == 0 and more:
                    scales(v)
                pair(PAIRS - 1, 0)

            def scales(v):
                pe.wait_ge(r_step, (v + 1) * R_STEPS)
                spread(v, R, r_psum, r_rows)

            def log_sums(v):
                pe.wait_ge(lse_dve, (v + 1) * LSE_STEPS)
                pe.wait_ge(blk_l, (v + 1) * PAIRS)
                spread(v, lse, lse_psum, lse_rows, 1)

            def unit(u, more):
                for k in range(NK + 1 if more else NK):
                    if k == 1 and more:
                        pe.wait_ge(f_in, (u + 2) * N_F * 16)
                    step(u, k if k < NK else None, u + 1, k - 1 if k >= 1 and more else None, more)
                if more:
                    log_sums(u + 1)

            norms(0)
            scales(0)
            pe.wait_ge(f_in, N_F * 16)
            for k in range(NK):
                step(0, None, 0, k)
            log_sums(0)
            with pe.Fori(0, UNITS - 1) as u:
                unit(u, True)
            unit(UNITS - 1, False)

        @block.scalar
        def _(act):
            act.add_instruction(mybir.InstLoadActFuncSet(name=nc.get_next_instruction_name(), engine=act.engine,
                                                         act_func_set_id=EXP_AND_LN))
            act.sem_inc(g_read, FREE)
            act.sem_inc(s_read, FREE)
            act.sem_inc(zh_made, FREE)
            act.sem_inc(o_read, 2 * FREE)
            act.sem_inc(lse_rows, 1)

            def high_features(u):
                act.wait_ge(x_in, (u + 1) * N_X * 16)
                if not (isinstance(u, int) and u == 0):
                    act.wait_ge(f_in, u * N_F * 16)
                    act.wait_ge(g_ready, u * NB)
                act.activation(LH[64:128, TW:TW * (TILES + 1)].rearrange("p (r w) -> p r w", w=PITCH)[:, :, 1:1 + HALF],
                               XP[64:128, :, 1:1 + SIDE:2], ACT.Copy).then_inc(h_inner, 1)
                act.wait_ge(h_inner, u + 1)
                act.activation(LH[64:128, PITCH:TW], LH[64:128, TILES * TW:TILES * TW + 2 * PITCH],
                               ACT.Copy).then_inc(h_made, 1)
                act.activation(LH[64:128, (TILES + 1) * TW:(TILES + 1) * TW + 2 * PITCH], LH[64:128, TW + PITCH:2 * TW],
                               ACT.Copy).then_inc(h_made, 1)

            def squares(u):
                act.wait_ge(x_in, (u + 1) * N_X * 16)
                if not (isinstance(u, int) and u == 0):
                    act.wait_ge(box_step, (u - 1) * BOX_STEPS + 2)
                act.sem_inc(act_gate, 1)
                for p, at, strip, n in ((0, TW, 0, (HT + 1) * STRIPS), (64, 0, (HT - 1) * STRIPS, (HT + 1) * STRIPS),
                                        (0, PITCH, (TILES - 1) * STRIPS, STRIPS - 1),
                                        (64, (HT + 1) * TW, 1, STRIPS - 1)):
                    act.activation(SQ[p:p + 64, at:at + n * PITCH].rearrange("p (r w) -> p r w", w=PITCH)[:, :, 1:1 + HALF],
                                   XP[64:128, strip:strip + n, 1:1 + SIDE:2], ACT.Square).then_inc(sq_made, 1)

            def read_rows(u, g, rows, made, read):
                act.wait_ge(made, u * GROUPS + g + 1)
                n = min(4, TILES - 4 * g) * TW
                act.activation(rows[:, 4 * g * TW:4 * g * TW + n], psM[0:TW, g % 2, 0:n], ACT.Copy).then_inc(read, 1)

            def high_blocks(u, g):
                if g == 0:
                    act.wait_ge(z_used, u * NB + ZFREE)
                act.wait_ge(blk_psum, u * PAIRS + g + 1)
                act.activation(Bh[:, g * 512:(g + 1) * 512], psM[0:TW, g % 2, :], ACT.Copy).then_inc(blk_h, 1)

            def score_pair(u, k, j):
                c0, n = cols(k, False)
                c = (u * NK + k) * TILES
                for par in range(FREE if k < NK - 1 else 1):
                    t = 2 * pair_of(k, j) + par
                    act.wait_ge(max_made, c + 2 * j + par + 1)
                    if par == 0 and not (isinstance(u, int) and u == 0):
                        act.wait_ge(z_made, (c + t + 1 - NB + TILES + 2) if k < NK - 1 else u * NB + 1)
                    act.activation(G[:, bass.ds(t * GLEN + c0, n)], psG[0:TW, par, 0:n], ACT.Copy).then_inc(g_read, 1)
                act.wait_ge(neg_made, (u * NK + k) * PAIRS + j + 1)
                for par in range(FREE):
                    t = 2 * pair_of(k, j) + par
                    v = S[:, par, :].rearrange("p (s w) -> p s w", w=PITCH)
                    parts = [v[:, 0:STRIPS * CHUNKS[k][1], 0:HALF]]
                    if k == NK - 1:
                        parts = [v[:, 0:5, 0:HALF], v[:, 6:8, 0:HALF]]
                    for m, e in enumerate(parts):
                        last = act.activation(e, e, ACT.Exp, bias=nm[:, bass.ds(k * TILES + t, 1)],
                                              accum_out=sg[:, bass.ds((k + m) * TILES + t, 1)])
                    last.then_inc(s_read, 1)

            def softmax_tile(u, k, t):
                c0, n = cols(k)
                i = (u * NK + k) * TILES + t
                act.wait_ge(arg_made, i + 2)
                act.sem_inc(act_gate, 1)
                y = G[:, bass.ds(t * GLEN + c0, n)]
                act.activation(y, y, ACT.Exp, bias=nb[:, bass.ds(u * TILES + t, 1)]).then_inc(y_made, 1)

            def high_pair(u, k, i, odd):
                n = cols(k)[1]
                z = (u * NK + k) * TILES + 2 * i
                slot = 2 * ((k + odd) % 2)
                act.wait_ge(z_used, z + 2)
                for j in range(2):
                    act.wait_ge(z_made, z + j + 2)
                    act.activation(Zh[:, slot + j, 0:n], Z[:, j, 0:n], ACT.Copy, scale=ZSCALE).then_inc(zh_made, 1)

            def read_out(u, k):
                c = u * NK + k
                n = cols(k)[1]
                act.wait_ge(z_used, (c + 1) * TILES + ZFREE)
                act.wait_ge(stored, (u * sum(N_OUT) + sum(N_OUT[:k]) + 1) * 16)
                for b in range(2):
                    act.activation(OSB[:, 0:n // PITCH, b:b + 2 * HALF + 1:2],
                                   psO[:, k % 2, b, 0:n].rearrange("p (s w) -> p s w", w=PITCH)[:, :, 0:HALF + 1],
                                   ACT.Copy, scale=0.25 / ZSCALE).then_inc(o_read, 1)

            def step(u, z, v, b, more=True):
                if z is None:
                    if b < NK - 1:
                        with act.Fori(0, PAIRS) as i:
                            score_pair(v, b, i)
                        return
                    for i in range(PAIRS):
                        score_pair(v, b, i)
                        for g in block_groups(i):
                            high_blocks(v, g)
                    return

                def pair(i, odd):
                    end = isinstance(i, int) and i == PAIRS - 1
                    if not end:
                        high_pair(u, z, i + 1, odd + 1)
                    elif z + 1 < NK:
                        high_pair(u, z + 1, 0, 0)
                    if z + 1 < NK:
                        softmax_tile(u, z + 1, 2 * i)
                        softmax_tile(u, z + 1, 2 * i + 1)
                    if b is not None:
                        score_pair(v, b, i)

                with act.Fori(0, PAIRS // 2 - 1) as i:
                    pair(2 * i, 0)
                    pair(2 * i + 1, 1)
                pair(PAIRS - 3, 0)
                if z == 0 and more:
                    scales(v)
                pair(PAIRS - 2, 1)
                if z == 0 and more:
                    for g in range(GROUPS):
                        read_rows(v, g, RB, r_psum, r_rows)
                pair(PAIRS - 1, 0)
                read_out(u, z)

            def scales(v):
                act.wait_ge(r_step, v * R_STEPS + 1)
                act.activation(lnn[:, :], nsq[:, :], ACT.Ln).then_inc(root_made, 1)
                act.wait_ge(root_made, 2 * v + 1)
                act.activation(root[:, :], lnn[:, :], ACT.Exp, scale=0.5).then_inc(root_made, 1)

            def log_sums(v, image):
                act.wait_ge(lse_dve, v * LSE_STEPS + 2)
                act.activation(ed[:, :], df[:, :], ACT.Exp).then_inc(lse_act, 1)
                act.wait_ge(lse_dve, v * LSE_STEPS + 4)
                act.activation(lns[:, :], tot[:, :], ACT.Ln).then_inc(lse_act, 1)
                if image:
                    squares(v + 1)

            def unit(u, more, image):
                for t in range(TILES):
                    if t % 2 == 0 and t // 2 < GROUPS:
                        read_rows(u, t // 2, BC, lse_psum, lse_rows)
                    if t == 2 * GROUPS:
                        act.wait_ge(lse_rows, (u + 1) * GROUPS + 1)
                        act.activation(BC[:, TILES * TW:CLEN], BC[:, PITCH:TW], ACT.Copy).then_inc(lse_wrap, 1)
                    if t == 6 and more:
                        high_features(u + 1)
                    softmax_tile(u, 0, t)
                high_pair(u, 0, 0, 0)
                for k in range(NK + 1 if more else NK):
                    step(u, k if k < NK else None, u + 1, k - 1 if k >= 1 and more else None, more)
                if more:
                    log_sums(u + 1, image)

            act.wait_ge(cleared, CLEARED)
            act.wait_ge(mask_ready, 1)
            squares(0)
            high_features(0)
            scales(0)
            for g in range(GROUPS):
                read_rows(0, g, RB, r_psum, r_rows)
            for k in range(NK):
                step(0, None, 0, k)
            log_sums(0, True)
            with act.Fori(0, UNITS - 2) as u:
                unit(u, True, True)
            unit(UNITS - 2, True, False)
            unit(UNITS - 1, False, False)

        def box_sums(eng, p0, p1, step, base):
            wide, tall = (TILES + 2) * TW, TILES * TW
            sq, bx = SQ[p0:p1, :], BX[p0:p1, :]
            eng.tensor_tensor(bx[:, 0:wide], sq[:, 0:wide], sq[:, 1:wide + 1], ALU.add).then_inc(step, 1)
            eng.wait_ge(step, base + 1)
            eng.tensor_tensor(bx[:, 0:wide], bx[:, 0:wide], sq[:, 2:wide + 2], ALU.add).then_inc(step, 1)
            eng.wait_ge(step, base + 2)
            eng.tensor_tensor(sq[:, 0:tall], bx[:, 0:tall], bx[:, TW:TW + tall], ALU.add).then_inc(step, 1)
            eng.wait_ge(step, base + 3)
            eng.tensor_tensor(sq[:, 0:tall], sq[:, 0:tall], bx[:, 2 * TW:2 * TW + tall], ALU.add).then_inc(step, 1)

        @block.vector
        def _(dve):
            for tile, value in ((XP[:, :, :], 0.0), (HL[:, :].bitcast(F32), 0.0), (LH[:, :].bitcast(F32), 0.0),
                                (H1[:, :].bitcast(F32), 0.0), (HV[:, :].bitcast(F32), 0.0), (ones[:, :], 1.0),
                                (SH[:, :, :], 0.0), (SHJ[:, :], 0.0), (SQ[0:64, :], 0.0)):
                dve.memset(tile, value).then_inc(cleared, 1)
            dve.sem_inc(zl_made, FREE)
            dve.sem_inc(arg_made, 1)
            dve.sem_inc(z_made, 1)
            dve.wait_ge(cleared, CLEARED)
            dve.memset(SQ[0:LAYERS, :], 0.0).then_inc(mask_step, 1)
            dve.wait_ge(mask_in, 32)
            dve.wait_ge(mask_step, 1)
            m = G[0:LAYERS, 0:SIDE * SIDE].rearrange("p (h w) -> p h w", w=SIDE)
            f = SQ[0:LAYERS, 0:FROWS * TW].rearrange("p (r j w) -> p j r w", j=STRIPS, w=PITCH)
            for j in range(STRIPS):
                lo, hi = max(TILES * j - 1, 0), min(TILES * j + TILES + 1, HALF)
                r = lo - (TILES * j - 1)
                last = dve.tensor_copy(f[:, j, r:r + hi - lo, 1:1 + HALF], m[:, 2 * lo:2 * hi:2, 0:SIDE:2])
            last.then_inc(mask_step, 1)
            dve.wait_ge(mask_step, 2)
            box_sums(dve, 0, LAYERS, mask_step, 2)
            dve.memset(G[:, :].rearrange("p (t c) -> p t c", c=GLEN)[:, :, 0:TW], 0.0)
            dve.wait_ge(mask_cols, 1)
            dve.memset(SQ[0:LAYERS, :], 0.0).then_inc(mask_ready, 1)
            dve.wait_ge(const_in, 32)
            dve.tensor_scalar(mmc[:, :, :], psM[0:TW, 0, 0:LAYERS * TILES].rearrange("p (t l) -> p l t", l=LAYERS),
                              0.0, None, ALU.is_equal).then_inc(mask_ready, 1)
            dve.wait_ge(mask_ready, 2)
            for layer in range(LAYERS):
                last = dve.tensor_tensor(mmc[:, layer, :], mmc[:, layer, :], vld[:, :], ALU.mult)
            last.then_inc(mask_ready, 1)
            dve.wait_ge(mask_ready, 3)
            for u in range(UNITS):
                at = slice(u * TILES, (u + 1) * TILES)
                dve.tensor_scalar(mm20[:, at], mmc[:, u // IMAGES, :], 20.0, None, ALU.mult).then_inc(mask_ready, 1)
                dve.tensor_scalar(nb[:, at], mmc[:, u // IMAGES, :], -1.0, BIG, ALU.add, ALU.mult).then_inc(mask_ready, 1)
            dve.tensor_scalar(big[:, :], vld[:, :], -2.0 * BIG, BIG, ALU.mult, ALU.add).then_inc(mask_ready, 1)
            dve.wait_ge(mask_ready, 3 + 2 * UNITS + 1)

            def low_features(u):
                dve.wait_ge(h_inner, u + 1)
                inner = lambda a: a[64:128, TW:TW * (TILES + 1)].rearrange("p (r w) -> p r w", w=PITCH)[:, :, 1:1 + HALF]
                dve.tensor_tensor(inner(HL), XP[64:128, :, 1:1 + SIDE:2], inner(LH), ALU.subtract).then_inc(l_inner, 1)
                dve.wait_ge(l_inner, u + 1)
                dve.tensor_copy(HL[64:128, PITCH:TW], HL[64:128, TILES * TW:TILES * TW + 2 * PITCH]).then_inc(l_made, 1)
                dve.tensor_copy(HL[64:128, (TILES + 1) * TW:(TILES + 1) * TW + 2 * PITCH],
                                HL[64:128, TW + PITCH:2 * TW]).then_inc(l_made, 1)

            def squared_norms(u):
                dve.wait_ge(norm_cols, u + 1)
                dve.tensor_scalar(nsq[:, :].rearrange("p (h t) -> p h t", t=HT), psM[0:TW, :, 0:HT], 1e-8, None,
                                  ALU.max).then_inc(r_step, 1)

            def scales(u):
                at = u * R_STEPS
                dve.wait_ge(root_made, 2 * (u + 1))
                dve.reciprocal(rcp[:, :], root[:, :]).then_inc(r_step, 1)
                dve.wait_ge(r_step, at + 2)
                dve.tensor_tensor(quo[:, :], nsq[:, :], rcp[:, :], ALU.mult).then_inc(r_step, 1)
                dve.wait_ge(r_step, at + 3)
                dve.tensor_tensor(nrm2[:, :], quo[:, :], root[:, :], ALU.add).then_inc(r_step, 1)
                dve.wait_ge(r_step, at + 4)
                dve.reciprocal(rcp[:, :], nrm2[:, :]).then_inc(r_step, 1)
                dve.wait_ge(r_step, at + 5)
                mm = mm20[:, bass.ds(u * TILES, TILES)]
                dve.tensor_tensor(R[:, :], rcp[:, :], mm, ALU.mult).then_inc(r_step, 1)
                dve.tensor_tensor(RA[:, bass.ds(u * TILES, TILES)], rcp[:, :], mm, ALU.mult).then_inc(r_step, 1)

            def low_blocks(u, g):
                dve.wait_ge(blk_h, u * PAIRS + g + 1)
                at = slice(g * 512, (g + 1) * 512)
                dve.tensor_tensor(Bl[:, at], psM[0:TW, g % 2, :], Bh[:, at], ALU.subtract).then_inc(blk_l, 1)

            def score_pair(u, k, j):
                s0, w = CHUNKS[k]
                n = w * TW
                c = (u * NK + k) * TILES
                for par in range(FREE):
                    dve.wait_ge(g_ready, c + 2 * j + par + 1)
                    dve.wait_ge(s_read, c + 2 * j + par + 1)
                    dve.sem_inc(dve_gate, 1)
                    dve.tensor_tensor_reduce(S[:, par, 0:n], psG[0:TW, par, 0:n], RB[:, s0 * TW:s0 * TW + n], 1.0, 0.0,
                                             ALU.mult, ALU.max, mx[:, par:par + 1]).then_inc(max_made, 1)
                dve.wait_ge(max_made, c + 2 * j + 2)
                dve.tensor_scalar(nm[:, bass.ds(k * TILES + 2 * pair_of(k, j), 2)], mx[:, :], -1.0, None,
                                  ALU.mult).then_inc(neg_made, 1)
                if k == NK - 1:
                    at = (2 * pair_of(k, j) + 1) * GLEN + cols(k)[0]
                    dve.wait_ge(g_read, c + 2 * j + 1 + FREE)
                    dve.sem_inc(dve_gate, 1)
                    dve.tensor_copy(G[:, bass.ds(at, n)], psG[0:TW, 1, 0:n]).then_inc(g_read, 1)

            def log_sums(u):
                at = u * LSE_STEPS
                by_tile = lambda a: a.rearrange("p (k t) -> p t k", t=TILES)
                dve.wait_ge(s_read, (u + 1) * NB + FREE)
                last = slice((NK - 1) * TILES, NK * TILES)
                dve.tensor_reduce(nM[:, :], by_tile(nm[:, :]), AX.X, ALU.min).then_inc(lse_dve, 1)
                dve.tensor_tensor(sg[:, last], sg[:, last], sg[:, NK * TILES:], ALU.add)
                dve.wait_ge(lse_dve, at + 1)
                dve.tensor_tensor(df[:, :].rearrange("p (k t) -> p k t", t=TILES),
                                  nM[:, :].unsqueeze(1).to_broadcast([TW, NK, TILES]),
                                  nm[:, :].rearrange("p (k t) -> p k t", t=TILES), ALU.subtract).then_inc(lse_dve, 1)
                dve.wait_ge(lse_act, u * 2 + 1)
                dve.tensor_tensor(df[:, :], ed[:, :], sg[:, 0:NK * TILES], ALU.mult).then_inc(lse_dve, 1)
                dve.wait_ge(lse_dve, at + 3)
                dve.tensor_reduce(tot[:, :], by_tile(df[:, :]), AX.X, ALU.add).then_inc(lse_dve, 1)
                dve.wait_ge(lse_act, u * 2 + 2)
                dve.tensor_tensor(tot[:, :], lns[:, :], nM[:, :], ALU.subtract).then_inc(lse_dve, 1)
                dve.wait_ge(lse_dve, at + 5)
                dve.tensor_tensor(lse[:, :], tot[:, :], big[:, :], ALU.max).then_inc(lse_dve, 1)

            def argument(u, k, t):
                c0, n = cols(k)
                g = G[:, bass.ds(t * GLEN + c0, n)]
                dve.scalar_tensor_tensor(out=g, in0=g, scalar=RA[:, bass.ds(u * TILES + t, 1)], in1=BC[:, c0 - TW:c0 - TW + n],
                                         op0=ALU.mult, op1=ALU.subtract).then_inc(arg_made, 1)

            def sum_pair(u, k, i):
                c0, n = cols(k)
                c = u * NK + k
                end = isinstance(i, int) and i == PAIRS - 1
                dve.wait_ge(y1_made, c * TILES + (TILES if end else 2 * i + 3) + SFREE)
                dve.wait_ge(zh_made, c * TILES + 2 * i + FREE)
                dve.wait_ge(zl_made, c * TILES + 2 * i + FREE)
                for j in range(2):
                    t = 0 if end and j == 1 else 2 * i + 1 + j
                    if end and j == 1:
                        dve.wait_ge(shj_in, (c + 1) * 16)
                        above = SHJ[:, 0:n]
                    else:
                        above = G[:, bass.ds((t - 1) * GLEN + c0 - TW, n)]
                    dve.tensor_tensor(Z[:, j, 0:n], G[:, bass.ds(t * GLEN + c0, n)], above, ALU.add).then_inc(z_made, 1)

            def low_pair(u, k, i, odd):
                n = cols(k)[1]
                slot = 2 * ((k + odd) % 2)
                for j in range(2):
                    dve.wait_ge(zh_made, (u * NK + k) * TILES + 2 * i + j + 1 + FREE)
                    dve.scalar_tensor_tensor(out=Zl[:, slot + j, 0:n], in0=Z[:, j, 0:n], scalar=ZSCALE,
                                             in1=Zh[:, slot + j, 0:n], op0=ALU.mult, op1=ALU.subtract).then_inc(zl_made, 1)

            def step(u, z, v, b, more=True):
                if z is None:
                    if b < NK - 1:
                        with dve.Fori(0, PAIRS) as i:
                            score_pair(v, b, i)
                        return
                    for i in range(PAIRS):
                        score_pair(v, b, i)
                        for g in block_groups(i):
                            low_blocks(v, g)
                    return

                def arguments(i):
                    if z + 1 < NK:
                        argument(u, z + 1, 2 * i)
                        argument(u, z + 1, 2 * i + 1)

                def pair(i, odd):
                    end = isinstance(i, int) and i == PAIRS - 1
                    low_pair(u, z, i, odd)
                    if b is None:
                        arguments(i)
                    if not end:
                        sum_pair(u, z, i + 1)
                    elif z + 1 < NK:
                        sum_pair(u, z + 1, 0)
                    if b is not None:
                        arguments(i)
                    if b is not None:
                        score_pair(v, b, i)

                with dve.Fori(0, PAIRS // 2 - 1) as i:
                    pair(2 * i, 0)
                    pair(2 * i + 1, 1)
                pair(PAIRS - 3, 0)
                if z == 0 and more:
                    squared_norms(v)
                pair(PAIRS - 2, 1)
                if z == 0 and more:
                    scales(v)
                pair(PAIRS - 1, 0)

            def unit(u, more):
                dve.wait_ge(lse_rows, u * GROUPS + 2)
                dve.wait_ge(wrap_made, u + 1)
                dve.sem_inc(dve_gate, 1)
                for t in range(TILES):
                    argument(u, 0, t)
                if more:
                    low_features(u + 1)
                sum_pair(u, 0, 0)
                dve.wait_ge(lse_wrap, u + 1)
                dve.sem_inc(dve_gate, 1)
                for k in range(NK + 1 if more else NK):
                    if k == 1 and more:
                        dve.wait_ge(r_rows, (u + 2) * GROUPS)
                        dve.sem_inc(dve_gate, 1)
                    step(u, k if k < NK else None, u + 1, k - 1 if k >= 1 and more else None, more)
                if more:
                    log_sums(u + 1)

            low_features(0)
            squared_norms(0)
            scales(0)
            dve.wait_ge(r_rows, GROUPS)
            dve.sem_inc(dve_gate, 1)
            for k in range(NK):
                step(0, None, 0, k)
            log_sums(0)
            with dve.Fori(0, UNITS - 1) as u:
                unit(u, True)
            unit(UNITS - 1, False)

        @block.gpsimd
        def _(pool):
            for tile in (SQ[64:128, :], BX[64:128, :]):
                pool.memset(tile, 0.0).then_inc(cleared, 1)
            pool.sem_inc(y1_made, SFREE)

            def row_sums(u):
                n = (HT + 2) * TW
                if not (isinstance(u, int) and u == 0):
                    pool.wait_ge(norm_cols, u)
                    pool.wait_ge(s_read, u * NB + FREE)
                pool.wait_ge(sq_made, (u + 1) * SQ_STEPS)
                pool.sem_inc(pool_gate, 1)
                pool.tensor_tensor(BX[:, 0:n], SQ[:, 0:n], SQ[:, 1:n + 1], ALU.add).then_inc(box_step, 1)
                pool.wait_ge(box_step, u * BOX_STEPS + 1)
                pool.tensor_tensor(BX[:, 0:n], BX[:, 0:n], SQ[:, 2:n + 2], ALU.add).then_inc(box_step, 1)

            def box_sums_of(u):
                n, at = HT * TW, (HT + 2) * TW
                pool.tensor_tensor(BX[:, at:at + n], BX[:, 0:n], BX[:, TW:TW + n], ALU.add).then_inc(box_step, 1)
                pool.wait_ge(box_step, u * BOX_STEPS + 3)
                pool.tensor_tensor(BX[:, at:at + n], BX[:, at:at + n], BX[:, 2 * TW:2 * TW + n],
                                   ALU.add).then_inc(box_step, 1)

            def wrap(u):
                pool.wait_ge(g_read, u * NB + TILES + FREE)
                pool.sem_inc(pool_gate, 1)
                g = G[:, :].rearrange("p (t c) -> p t c", c=GLEN)
                pool.tensor_copy(g[:, :, GLEN - WRAP:GLEN], g[:, :, TW + PITCH:2 * TW]).then_inc(wrap_made, 1)

            def sum_y1(u, k, t, j, i):
                c0, n = cols(k)
                slot = (2 * k + j) % SFREE
                pool.wait_ge(sh_in[slot], (u * (NB // SFREE) + (k * TILES + j) // SFREE + i + 1) * 16)
                g = G[:, bass.ds(t * GLEN + c0, n)]
                pool.tensor_tensor(g, g, SH[:, slot, 0:n], ALU.add).then_inc(y1_made, 1)

            def unit(u, more, image):
                for k in range(NK):
                    with pool.Fori(0, PAIRS // 2) as i:
                        for j in range(4):
                            sum_y1(u, k, 4 * i + j, j, i)
                    for j in range(2):
                        sum_y1(u, k, TILES - 2 + j, j, PAIRS // 2)
                    if k == 0 and more:
                        pool.wait_ge(y1_made, u * NB + TILES + SFREE)
                        box_sums_of(u + 1)
                        pool.wait_ge(box_step, (u + 2) * BOX_STEPS)
                        pool.sem_inc(pool_gate, 1)
                if more:
                    pool.wait_ge(y1_made, (u + 1) * NB + SFREE)
                    pool.wait_ge(z_made, (u + 1) * NB + 1)
                    wrap(u + 1)
                if image:
                    pool.wait_ge(wrap_made, u + 2)
                    row_sums(u + 2)
                    pool.wait_ge(box_step, (u + 2) * BOX_STEPS + 2)
                    pool.sem_inc(pool_gate, 1)

            pool.wait_ge(cleared, CLEARED)
            row_sums(0)
            pool.wait_ge(box_step, 2)
            box_sums_of(0)
            pool.wait_ge(box_step, BOX_STEPS)
            pool.sem_inc(pool_gate, 1)
            wrap(0)
            pool.wait_ge(wrap_made, 1)
            row_sums(1)
            pool.wait_ge(box_step, BOX_STEPS + 2)
            pool.sem_inc(pool_gate, 1)
            with pool.Fori(0, UNITS - 2) as u:
                unit(u, True, True)
            unit(UNITS - 2, True, False)
            unit(UNITS - 1, False, False)


def kernel(x, L0_conv_mask, L1_conv_mask):
    import numpy as np
    import concourse.bacc as bacc
    from concourse.bass_utils import run_bass_kernel_spmd

    nc = bacc.Bacc("TRN2", target_bir_lowering=False, num_devices=1)
    rows = np.arange(TW) // PITCH * TILES
    valid = (rows[:, None] + np.arange(TILES)[None, :] < HALF) & (np.arange(TW) % PITCH < HALF)[:, None]
    arrays = {
        "x": np.ascontiguousarray(x),
        "mask0": np.ascontiguousarray(L0_conv_mask),
        "mask1": np.ascontiguousarray(L1_conv_mask),
        "ident": np.eye(128, dtype=np.float32),
        "valid": valid.astype(np.float32),
    }
    ins = [nc.dram_tensor(n, a.shape, mybir.dt.from_np(a.dtype), kind="ExternalInput").ap() for n, a in arrays.items()]
    out = nc.dram_tensor("out", (IMAGES, C, SIDE, SIDE), F32, kind="ExternalOutput").ap()
    contextual_attention(nc, *ins, out)
    return run_bass_kernel_spmd(nc, [arrays], core_ids=[0]).results[0]["out"]
```
